# Optimizing a Trainium2 kernel written in Bass

```python
import numpy as np
import jax
import jax.numpy as jnp

def _softmax(x, axis=-1):
    return jax.nn.softmax(x, axis=axis)

def _gelu(x):
    return jax.nn.gelu(x, approximate=True)

def _silu(x):
    return jax.nn.silu(x)

def _sigmoid(x):
    return jax.nn.sigmoid(x)

def _layernorm(x, axis=-1, eps=1e-05):
    m = jnp.mean(x, axis=axis, keepdims=True)
    v = jnp.var(x, axis=axis, keepdims=True)
    return (x - m) / jnp.sqrt(v + eps)

def _scatter_add(tgt, idx, src, axis=0):
    return tgt.at[idx].add(src)

def _segment_sum(src, seg, n):
    return jax.ops.segment_sum(src, seg, n)
kernel_name = 'mk_macaron_d1_jaxref_r8_251d3d'

def setup_inputs(seed: int=0):
    np.random.seed(seed)
    _w = jnp.asarray

    def _L0_attn_setup():
        import jax, jax.numpy as jnp
        import numpy as np
        B, T, C, H = (2, 256, 128, 16)
        R = 32
        LORA_SCALE = 0.5
        HD = C // H

        def lora_linear(x, w, b, la, lb):
            return x @ w.T + b + LORA_SCALE * (x @ la.T @ lb.T)
        key = jax.random.key(seed)
        ks = jax.random.split(key, 8)
        std = 0.02
        return {'x': jax.random.normal(ks[0], (B, T, C), jnp.float32), 'w_attn': jax.random.normal(ks[1], (3 * C, C), jnp.float32) * std, 'b_attn': jnp.zeros((3 * C,), jnp.float32), 'la_attn': jax.random.normal(ks[2], (R, C), jnp.float32) * std, 'lb_attn': jax.random.normal(ks[3], (3 * C, R), jnp.float32) * std, 'w_proj': jax.random.normal(ks[4], (C, C), jnp.float32) * std, 'b_proj': jnp.zeros((C,), jnp.float32), 'la_proj': jax.random.normal(ks[5], (R, C), jnp.float32) * std, 'lb_proj': jax.random.normal(ks[6], (C, R), jnp.float32) * std}
    _L0_attn_in = _L0_attn_setup()

    def _L0_ffn_setup():
        import jax, jax.numpy as jnp
        import numpy as np
        NUM_EXPERTS = 8
        IN_FEATURES = 128
        HIDDEN_FEATURES = 512
        GATE_DIM = 16
        EPS = 0.0001
        key = jax.random.key(seed)
        ks = jax.random.split(key, 7)
        hidden_states = jax.random.normal(ks[0], (1, 256, IN_FEATURES), dtype=jnp.float32)
        wg_red = jax.random.normal(ks[1], (GATE_DIM, IN_FEATURES), dtype=jnp.float32) * 0.02
        wg = jax.random.normal(ks[2], (NUM_EXPERTS, GATE_DIM), dtype=jnp.float32)
        w1 = jax.random.uniform(ks[3], (NUM_EXPERTS, IN_FEATURES, HIDDEN_FEATURES), dtype=jnp.float32)
        b1 = jax.random.uniform(ks[4], (NUM_EXPERTS, HIDDEN_FEATURES), dtype=jnp.float32)
        w2 = jax.random.uniform(ks[5], (NUM_EXPERTS, HIDDEN_FEATURES, IN_FEATURES), dtype=jnp.float32)
        b2 = jax.random.uniform(ks[6], (NUM_EXPERTS, IN_FEATURES), dtype=jnp.float32)
        return {'hidden_states': hidden_states, 'wg_red': wg_red, 'wg': wg, 'w1': w1, 'b1': b1, 'w2': w2, 'b2': b2}
    _L0_ffn_in = _L0_ffn_setup()
    _d = {'L0_attn_x': _L0_attn_in['x'], 'L0_attn_w_attn': _L0_attn_in['w_attn'], 'L0_attn_b_attn': _L0_attn_in['b_attn'], 'L0_attn_la_attn': _L0_attn_in['la_attn'], 'L0_attn_lb_attn': _L0_attn_in['lb_attn'], 'L0_attn_w_proj': _L0_attn_in['w_proj'], 'L0_attn_b_proj': _L0_attn_in['b_proj'], 'L0_attn_la_proj': _L0_attn_in['la_proj'], 'L0_attn_lb_proj': _L0_attn_in['lb_proj'], 'L0_ffn_wg_red': _L0_ffn_in['wg_red'], 'L0_ffn_wg': _L0_ffn_in['wg'], 'L0_ffn_w1': _L0_ffn_in['w1'], 'L0_ffn_b1': _L0_ffn_in['b1'], 'L0_ffn_w2': _L0_ffn_in['w2'], 'L0_ffn_b2': _L0_ffn_in['b2']}
    _x0 = _d['L0_attn_x']
    _d['L0_attn_x'] = jax.random.normal(jax.random.fold_in(jax.random.key(seed), 1), (4, 1024, 128), dtype=_x0.dtype)
    del _x0
    return _d

def reference(L0_attn_x, L0_attn_w_attn, L0_attn_b_attn, L0_attn_la_attn, L0_attn_lb_attn, L0_attn_w_proj, L0_attn_b_proj, L0_attn_la_proj, L0_attn_lb_proj, L0_ffn_wg_red, L0_ffn_wg, L0_ffn_w1, L0_ffn_b1, L0_ffn_w2, L0_ffn_b2):

    def _L0_attn_ref(x, w_attn, b_attn, la_attn, lb_attn, w_proj, b_proj, la_proj, lb_proj):
        import jax, jax.numpy as jnp
        import numpy as np
        B, T, C, H = (2, 256, 128, 16)
        R = 32
        LORA_SCALE = 0.5
        HD = C // H

        def lora_linear(x, w, b, la, lb):
            return x @ w.T + b + LORA_SCALE * (x @ la.T @ lb.T)
        Bsz, Tlen, Cdim = x.shape
        qkv = lora_linear(x, w_attn, b_attn, la_attn, lb_attn)
        q, k, v = jnp.split(qkv, 3, axis=2)
        rs = lambda t: t.reshape(Bsz, Tlen, H, HD).transpose(0, 2, 1, 3)
        q, k, v = (rs(q), rs(k), rs(v))
        att = jnp.einsum('bhqd,bhkd->bhqk', q, k) * (1.0 / np.sqrt(HD))
        causal = jnp.tril(jnp.ones((Tlen, Tlen), dtype=bool))
        att = jnp.where(causal[None, None], att, -jnp.inf)
        att = jax.nn.softmax(att, axis=-1)
        y = jnp.einsum('bhqk,bhkd->bhqd', att, v)
        y = y.transpose(0, 2, 1, 3).reshape(Bsz, Tlen, Cdim)
        return lora_linear(y, w_proj, b_proj, la_proj, lb_proj)

    def _L0_ffn_ref(hidden_states, wg_red, wg, w1, b1, w2, b2):
        import jax, jax.numpy as jnp
        import numpy as np
        NUM_EXPERTS = 8
        IN_FEATURES = 128
        HIDDEN_FEATURES = 512
        GATE_DIM = 16
        EPS = 0.0001
        b, t, c = hidden_states.shape
        x = hidden_states.reshape(-1, c)
        xr = x @ wg_red.T
        wg_unit = wg / jnp.maximum(jnp.linalg.norm(wg, axis=1, keepdims=True), EPS)
        logits = xr @ wg_unit.T
        gates = jax.nn.softmax(logits, axis=1)
        indices_s = jnp.argmax(gates, axis=1)
        scores = jnp.max(gates, axis=1)
        E = wg.shape[0]
        out = jnp.zeros_like(x)
        for e in range(E):
            mask = (indices_s == e).astype(x.dtype)[:, None]
            h = jax.nn.gelu(x @ w1[e] + b1[e], approximate=False)
            out = out + mask * (h @ w2[e] + b2[e])
        out = out * scores[:, None]
        return out.reshape(b, t, c)
    x = L0_attn_x
    x = x + 0.5 * _L0_ffn_ref(_layernorm(x, axis=-1), L0_ffn_wg_red, L0_ffn_wg, L0_ffn_w1, L0_ffn_b1, L0_ffn_w2, L0_ffn_b2)
    x = x + _L0_attn_ref(_layernorm(x, axis=-1), L0_attn_w_attn, L0_attn_b_attn, L0_attn_la_attn, L0_attn_lb_attn, L0_attn_w_proj, L0_attn_b_proj, L0_attn_la_proj, L0_attn_lb_proj)
    x = x + 0.5 * _L0_ffn_ref(_layernorm(x, axis=-1), L0_ffn_wg_red, L0_ffn_wg, L0_ffn_w1, L0_ffn_b1, L0_ffn_w2, L0_ffn_b2)
    return x

_drawn_inputs = setup_inputs


def setup_inputs(seed=0):
    import zlib

    import numpy as np

    out = dict(_drawn_inputs(seed))
    spreads = {'L0_attn_b_attn': (0.0, 0.8), 'L0_attn_b_proj': (0.0, 1.657)}
    factors = {'L0_attn_w_attn': 8.0,
     'L0_attn_la_attn': 8.0,
     'L0_attn_lb_attn': 8.0,
     'L0_attn_w_proj': 8.0,
     'L0_attn_la_proj': 8.0,
     'L0_attn_lb_proj': 8.0,
     'L0_ffn_b1': 4.024,
     'L0_ffn_b2': 22.454}
    for name, (base, spread) in spreads.items():
        noise = np.random.default_rng([zlib.crc32(name.encode()), seed]).standard_normal(out[name].shape)
        drawn = base * np.exp(spread * noise) if base else spread * noise
        out[name] = jnp.asarray(drawn.astype(out[name].dtype))
    for name, factor in factors.items():
        out[name] = (out[name] * factor).astype(out[name].dtype)
    return out
```

```python
from contextlib import ExitStack

import concourse.bass as bass
from concourse import mybir

P = 128
ALU = mybir.AluOpType
ACT = mybir.ActivationFunctionType
F32 = mybir.dt.float32
BF16 = mybir.dt.bfloat16
I32 = mybir.dt.int32
U32 = mybir.dt.uint32
AX_X = mybir.AxisListType.X

LN_EPS = 1e-5
NORM_EPS = 1e-4
LORA_SCALE = 0.5
BRANCH = 0.5
LOWEST = -3.0e38
HEADS = 16
G4 = 4
DMA = 16

Q_PARTS = (0, 0, 0, 1, 1, 2)
K_PARTS = (0, 1, 2, 0, 1, 0)


def macaron_kernel(nc, x, w_attn, b_attn, la_attn, lb_attn, w_proj, b_proj, la_proj, lb_proj,
                   wg_red, wg, w1, b1, w2, b2, out):
    B, T, C = x.shape
    N = B * T
    NT = N // P
    NG = NT // G4
    E, _, F = w1.shape
    FK = F // P
    GD = wg.shape[1]
    R = la_attn.shape[0]
    NS = NT + E - 1
    HD = C // HEADS
    SCALE = float(HD) ** -0.5
    QUADS = HEADS // 4
    QT = T // P
    CW = 512
    NCH = T // CW
    DIAG = CW // P
    SR = 6 * HD
    KR = SR + 3
    STEPS = [(c, j) for c in range(NCH) for j in range(DIAG * (c + 1))]
    NSTEP = len(STEPS)
    CHUNKS = [(i, kc, pr, hh) for i in range(QT) for kc in range(i // DIAG + 1) for pr in range(2) for hh in range(2)]
    NP1 = len(CHUNKS)
    P1_STEPS = 8
    P1_PER = NP1 // P1_STEPS
    NQ = B * QUADS
    PRING = 3
    assert C == P and NP1 % P1_STEPS == 0 and NSTEP % PRING == 0 and NT % 8 == 0

    def diag(t):
        c, j = STEPS[t]
        return j >= DIAG * c

    def width(t):
        c, j = STEPS[t]
        return CW - P * max(0, j - DIAG * c)

    NDIAG = sum(diag(t) for t in range(NSTEP))

    with ExitStack() as ctx:
        def sb(name, shape, dt):
            return ctx.enter_context(nc.sbuf_tensor(name, shape, dt))

        def sem(name):
            return ctx.enter_context(nc.semaphore(name))

        def dram(name, shape, dt):
            return nc.dram_tensor(name, shape, dt, kind="Internal").ap()

        ps = ctx.enter_context(nc.psum_tensor("ps", [P, 8, 512], F32))

        x_sb = sb("x_sb", [P, NT, C], F32)
        z_sb = sb("z_sb", [P, NT, C], F32)
        zT = sb("zT", [P, N], F32)
        w1_sb = sb("w1_sb", [P, E, F], F32)
        w2_sb = sb("w2_sb", [P, E, FK, C], F32)
        b1_rows = sb("b1_rows", [P, E * F], BF16)
        b2_rows = sb("b2_rows", [P, E * C], BF16)
        w_all = sb("w_all", [P, 4 * C], F32)
        wgate = sb("wgate", [P, E], F32)
        b_qkv = sb("b_qkv", [P, 3], F32)
        bv_all = sb("bv_all", [P, C], F32)
        bp_all = sb("bp_all", [P, C], F32)

        ident = sb("ident", [P, P], F32)
        ones_bf = sb("ones_bf", [P, P], BF16)
        before = sb("before", [P, P], BF16)
        causal = sb("causal", [P, 512], F32)
        rev = sb("rev", [P, E], F32)
        minus_half = sb("minus_half", [P, NT], F32)
        starts = sb("starts", [1, NS], F32)

        stats = sb("stats", [P, NT, 6], F32)
        lnw = sb("lnw", [P, 6, NT], F32)
        mean = sb("mean", [P, NT], F32)
        rstd = sb("rstd", [P, NT], F32)
        logit = sb("logit", [P, NT, E], F32)
        gtmp = sb("gtmp", [P, NT, E], F32)
        slot_of = sb("slot_of", [P, NT, E], F32)
        gexp = sb("gexp", [P, NT, E], F32)
        gmax = sb("gmax", [P, 3, NT], F32)
        score = sb("score", [P, NT], F32)
        onehot = sb("onehot", [P, NT, E], BF16)
        scanA = sb("scanA", [P, NT // 2 + NT, E], F32)
        scanB = sb("scanB", [P, NT // 2 + NT, E], F32)
        cnt_i = sb("cnt_i", [P, 2, E], I32)
        padA = sb("padA", [P, E // 2 + E], F32)
        padB = sb("padB", [P, E // 2 + E], F32)
        ebase = sb("ebase", [P, E], F32)
        pos_f = sb("pos_f", [P, NT], F32)
        pos = sb("pos", [P, NT], I32)
        ecmp = sb("ecmp", [1, NS, E - 1], F32)
        etab_f = sb("etab_f", [1, NS], F32)
        etab = sb("etab", [1, NS], I32)

        AW = 2 * (4 * 2 * T // 2) + 4 * QT * P + PRING * 4 * CW
        arena = sb("arena", [P, AW], F32)

        def carve(at, words):
            assert at + words <= AW
            return arena[:, at:at + words], at + words

        gath, at = carve(0, NT * C)
        xin, at = carve(at, 4 * C)
        xs, at = carve(at, 2 * P)
        hid, at = carve(at, 2 * F)
        hT, at = carve(at, 2 * F)
        yr, at = carve(at, 4 * C)
        gath = gath.rearrange("p (a c) -> p a c", a=NT)
        xin = xin.rearrange("p (r c) -> p r c", r=4)
        xs = xs.rearrange("p (r c) -> p r c", r=2)
        hid = hid.rearrange("p (r c) -> p r c", r=2)
        hT = hT.rearrange("p (r k c) -> p r k c", r=2, k=FK)
        yr = yr.rearrange("p (r c) -> p r c", r=4)

        q_stk, at = carve(0, 4 * 2 * T // 2)
        k_stk, at = carve(at, 4 * 2 * T // 2)
        v_aug, at = carve(at, 4 * QT * P)
        prob, _ = carve(at, PRING * 4 * CW)
        vf, at = carve(at, 2 * CW)
        rf, at = carve(at, 2 * CW)
        parts, at = carve(at, 3 * CW)
        q_stk = q_stk.bitcast(BF16).rearrange("p (s r t) -> p s r t", s=4, r=2)
        k_stk = k_stk.bitcast(BF16).rearrange("p (s r t) -> p s r t", s=4, r=2)
        v_aug = v_aug.rearrange("p (s j h d) -> p s j h d", s=4, j=QT, h=4)
        prob = prob.rearrange("p (s g h n) -> p s g h n", s=PRING, g=2, h=2)
        vf = vf.rearrange("p (r n) -> p r n", r=2)
        rf = rf.rearrange("p (r n) -> p r n", r=2)
        parts = parts.bitcast(BF16).rearrange("p (r s n) -> p r s n", r=2, s=3)

        v_all = sb("v_all", [P, NT, C], F32)
        yraw = sb("yraw", [P, NCH, CW], F32)
        rden = sb("rden", [P, DIAG, 4], F32)
        junk = sb("junk", [P, 2, 512], BF16)
        mx = sb("mx", [P, 4, QT], F32)
        mx0 = sb("mx0", [P, 4, QT], F32)
        nm = sb("nm", [4 * QT, 3, P], F32)
        nm_parts = sb("nm_parts", [4 * QT, 3, P], BF16)

        wattn_in, at = carve(at, 3 * C)
        la_in, at = carve(at, C)
        lb_in, at = carve(at, 3 * R)
        wproj_in, at = carve(at, C)
        lap_in, at = carve(at, C)
        lbp_in, at = carve(at, R)
        lbT, at = carve(at, 4 * C)
        wattn_in = wattn_in.rearrange("p (j c) -> p j c", j=3)
        lb_in = lb_in.rearrange("p (j r) -> p j r", j=3)
        la_in, lap_in, lbT = la_in[0:R], lap_in[0:R], lbT[0:R]
        wgred_in = sb("wgred_in", [GD, C], F32)
        wg_in = sb("wg_in", [E, GD], F32)
        wg_sq = sb("wg_sq", [E, GD], F32)
        wg_n = sb("wg_n", [E, 3], F32)
        wg_unit = sb("wg_unit", [E, GD], F32)
        wgT = sb("wgT", [GD, E], F32)
        BF_W = E * (F + C) // P
        bias_in = sb("bias_in", [P, BF_W], F32)
        bias_r = sb("bias_r", [P, 2, BF_W], F32)
        bias_parts = sb("bias_parts", [P, 3, BF_W], BF16)

        slots = dram("slots", [NS * P, C], F32)
        yslots = dram("yslots", [NS * P, C], F32)
        bias_d = dram("bias_d", [3, E * (F + C)], BF16)
        stack_d = dram("stack_d", [2, HEADS, SR, N], BF16)
        nm_d = dram("nm_d", [3, 4 * QT, P], BF16)
        x_dram = x.rearrange("b t c -> (b t) c").rearrange("(a p) c -> p a c", p=P)
        out_dram = out.rearrange("b t c -> (b t) c").rearrange("(a p) c -> p a c", p=P)
        BW1 = E * F // P

        block = ctx.enter_context(nc.Block())
        TILE_STEPS = NS + 3
        FIRST = 8
        LAST = FIRST + 4 * ((NS - FIRST) // 4)

        def tile_steps(eng, step):
            for s in range(FIRST):
                step(s, s % 4, s // 4)
            with eng.Fori(FIRST // 4, LAST // 4) as turn:
                for r in range(4):
                    step(turn * 4 + r, r, turn)
            for s in range(LAST, TILE_STEPS):
                step(s, s % 4, s // 4)

        def runs(s, lag):
            return not isinstance(s, int) or 0 <= s - lag < NS

        def later(s, lag):
            return not isinstance(s, int) or s - lag >= 0

        def per_ring(r):
            return (NS - r + 3) // 4

        x_in = [sem(f"x_in{g}") for g in range(4)]
        w1_in, w2_in, small_in, gate_in, bias_i, bias_out, bias_back = (
            sem(n) for n in ("w1_in", "w2_in", "small_in", "gate_in", "bias_i", "bias_out", "bias_back"))
        consts, zeros_done, slots_clear = sem("consts"), sem("zeros_done"), sem("slots_clear")
        CONSTS = 16
        bn_done, etab_done, root_in, root_done = sem("bn_done"), sem("etab_done"), sem("root_in"), sem("root_done")
        dve = sem("dve")
        wprep_pe, wprep_got = sem("wprep_pe"), sem("wprep_got")
        bias_split = sem("bias_split")
        z_ready, zt_put, zt_got = sem("z_ready"), sem("zt_put"), sem("zt_got")
        logits_done, gate_sub, gate_exp, onehot_done, counted, pos_done = (
            sem(n) for n in ("logits_done", "gate_sub", "gate_exp", "onehot_done", "counted", "pos_done"))
        scattered = sem("scattered")
        slot_in = [sem(f"slot_in{r}") for r in range(4)]
        xt_put, xt_got, up_done, gelu_done, ht_put, ht_got, down_done, y_got = (
            sem(n) for n in ("xt_put", "xt_got", "up_done", "gelu_done", "ht_put", "ht_got", "down_done", "y_got"))
        y_out = [sem(f"y_out{r}") for r in range(4)]
        gathered = [sem(f"gathered{g}") for g in range(4)]
        moe_added, out_done = sem("moe_added"), sem("out_done")

        SMALL_LOADS = 9
        wt_put, wt_got = sem("wt_put"), sem("wt_got")
        qk_put, v32_got, hi_got, rest_got, mid_got, parts_done = (
            sem(n) for n in ("qk_put", "v32_got", "hi_got", "rest_got", "mid_got", "parts_done"))
        qk_out = [sem("q_out"), sem("k_out")]
        v_mul, v_got, k_ones, v_ones = sem("v_mul"), sem("v_got"), sem("k_ones"), sem("v_ones")
        stack_in = [sem(f"stack_in{s}") for s in range(4)]
        quad_free, vaug_in = sem("quad_free"), sem("vaug_in")
        max_mul, max_free, max_done, max_put, misc_free = (
            sem(n) for n in ("max_mul", "max_free", "max_done", "max_put", "misc_free"))
        nm_dve, nm_done, nm_out, nm_in = sem("nm_dve"), sem("nm_done"), sem("nm_out"), sem("nm_in")
        score_mul = [sem("score_mulA"), sem("score_mulB")]
        exp_done = [sem("exp_doneA"), sem("exp_doneB")]
        causal_done, prob_free, pv_free, yraw_free, rden_done = (
            sem(n) for n in ("causal_done", "prob_free", "pv_free", "yraw_free", "rden_done"))
        y_ready, yt_put, yt_got, proj_mul, proj_sum, att_added = (
            sem(n) for n in ("y_ready", "yt_put", "yt_got", "proj_mul", "proj_sum", "att_added"))
        passed, passed_pool = sem("passed"), sem("passed_pool")
        OUT_RUN = 6 * DMA
        NQK = N // CW

        def quads(eng, quad):
            with eng.Fori(0, B - 1) as b:
                for r in range(QUADS):
                    quad(b, r, b * QUADS + r, False)
            for r in range(QUADS):
                quad(B - 1, r, (B - 1) * QUADS + r, True)

        def has(r, last, ahead):
            return not last or r + ahead < QUADS

        def qk_chunks(eng, chunk):
            for w in range(2):
                chunk(0, w, True)
            with eng.Fori(1, NQK) as n:
                for w in range(2):
                    chunk(n, w, False)

        def attention_sp(sp):
            def store(n, w, first):
                sp.wait_ge(parts_done, n * 2 + (w + 1))
                for k in range(6):
                    part = (Q_PARTS, K_PARTS)[w][k]
                    sp.dma_start(stack_d[w, :, HD * k:HD * (k + 1), bass.ds(n * CW, CW)], parts[:, w, part, :]).then_inc(qk_out[w], DMA)

            qk_chunks(sp, store)
            for w in range(2):
                sp.wait_ge(qk_out[w], NQK * OUT_RUN)
            sp.wait_ge(k_ones, 1)

            def load_stack(b, r, u):
                sp.wait_ge(quad_free, u + 1)
                for w, stk in ((0, q_stk), (1, k_stk)):
                    for half in range(2):
                        src = stack_d[w, 4 * r + half:4 * r + half + 3:2, :, bass.ds(b * T, T)].rearrange("h s t -> s h t")
                        sp.dma_start(stk[64 * half:64 * half + SR, r, :, :], src).then_inc(stack_in[r], DMA)

            def pass_maxima(r, u):
                sp.wait_ge(nm_done, u + 1)
                if not isinstance(u, int) or u > 0:
                    sp.wait_ge(nm_in, u * 2 * DMA)
                sp.dma_start(nm_d.rearrange("s m q -> m s q"), nm_parts[:]).then_inc(nm_out, DMA)
                sp.wait_ge(nm_out, (u + 1) * DMA)
                rows = nm_d.rearrange("s (g h i) q -> h s g (i q)", g=2, h=2)
                for half in range(2):
                    sp.dma_start(q_stk[64 * half + SR:64 * half + KR, r, :, :], rows[half]).then_inc(nm_in, DMA)

            load_stack(0, 0, 0)
            load_stack(0, 1, 1)
            pass_maxima(0, 0)

            def quad(b, r, u, last):
                if has(r, last, 2):
                    load_stack(b + (r + 2) // QUADS, (r + 2) % QUADS, u + 2)
                if has(r, last, 1):
                    pass_maxima((r + 1) % QUADS, u + 1)
            quads(sp, quad)

        def attention_pool(pool):
            pool.wait_ge(moe_added, NT)
            pool.memset(k_stk[:], 1.0).then_inc(k_ones, 1)
            pool.memset(v_aug[:], 1.0).then_inc(v_ones, 1)

            def middle(n, w, first):
                pool.wait_ge(rest_got, n * 2 + (w + 1))
                if not first:
                    pool.wait_ge(qk_out[w], n * OUT_RUN)
                pool.sem_inc(passed_pool, 1)
                pool.tensor_copy(parts[:, w, 1, :], rf[:, w, :]).then_inc(mid_got, 1)
            qk_chunks(pool, middle)
            pool.wait_ge(v_got, NG)
            pool.wait_ge(v_ones, 1)

            def values(b, r, u):
                pool.wait_ge(quad_free, u + 1)
                pool.sem_inc(passed_pool, 1)
                pool.tensor_copy(v_aug[:, r, :, :, 0:HD],
                                 v_all[:, bass.ds(b * QT, QT), r * 4 * HD:(r + 1) * 4 * HD].rearrange("p j (h d) -> p j h d", h=4)).then_inc(vaug_in, 1)
            values(0, 0, 0)

            def quad(b, r, u, last):
                if has(r, last, 1):
                    values(b + (r + 1) // QUADS, (r + 1) % QUADS, u + 1)
                for t in range(NSTEP):
                    if diag(t):
                        for g in range(2):
                            pool.wait_ge(exp_done[g], u * NSTEP + (t + 1))
                            pool.sem_inc(passed_pool, 1)
                            tri = prob[:, t % PRING, g, :, 0:P]
                            pool.affine_select(out=tri, in_=tri, compare_op=ALU.is_ge, fill=0.0, base=0,
                                               pattern=[[0, 2], [1, P]], channel_multiplier=-1).then_inc(causal_done, 1)
            quads(pool, quad)

        def attention_act(act):
            act.wait_ge(small_in, SMALL_LOADS * DMA)

            def high(n, w, first):
                act.wait_ge(qk_put, n * 2 + (w + 1))
                if not first:
                    act.wait_ge(parts_done, n * 2 + (w - 1))
                    act.wait_ge(qk_out[w], n * OUT_RUN)
                act.activation(vf[:, w, :], ps[:, 2 + w, :], ACT.Identity, bias=b_qkv[:, w:w + 1]).then_inc(v32_got, 1)
                act.wait_ge(v32_got, n * 2 + (w + 1))
                act.copy(parts[:, w, 0, :], vf[:, w, :]).then_inc(hi_got, 1)
            qk_chunks(act, high)

            def quad(b, r, u, last):
                for t in range(NSTEP):
                    n = width(t)
                    for g in range(2):
                        act.wait_ge(score_mul[g], u * NSTEP + (t + 1))
                        act.wait_ge(prob_free, u * NSTEP + (t + 1))
                        act.activation(prob[:, t % PRING, g, :, 0:n], ps[:, 2 * g:2 * g + 2, 0:n], ACT.Exp,
                                       scale=SCALE).then_inc(exp_done[g], 1)
            quads(act, quad)

            for g in range(NG):
                act.wait_ge(yt_put, g + 1)
                act.copy(zT[:, g * 512:(g + 1) * 512], ps[:, g % 2, :]).then_inc(yt_got, 1)

        def prepare_attention(v, put, own):
            v.wait_ge(wt_put, 1)
            put(v.tensor_copy(w_all[:], ps[:, 6, :]))
            v.tensor_copy(lbT[:], ps[0:R, 7, :]).then_inc(wt_got, 1)
            v.wait_ge(wt_put, 2)
            own()
            v.scalar_tensor_tensor(out=w_all[:], in0=ps[:, 6, :], scalar=LORA_SCALE, in1=w_all[:],
                                   op0=ALU.mult, op1=ALU.add).then_inc(wt_got, 1)

        def attention_dve(v):
            for g in range(NG):
                v.wait_ge(v_mul, g + 1)
                v.tensor_tensor(v_all[:, G4 * g:G4 * (g + 1), :], ps[:, 4 + g % 2, :].rearrange("p (a c) -> p a c", a=G4),
                                bv_all[:].unsqueeze(1).broadcast_to([P, G4, C]), ALU.add).then_inc(v_got, 1)

            def rest(n, w, first):
                v.wait_ge(hi_got, n * 2 + (w + 1))
                v.tensor_tensor(rf[:, w, :], vf[:, w, :], parts[:, w, 0, :], ALU.subtract).then_inc(rest_got, 1)
                v.wait_ge(mid_got, n * 2 + (w + 1))
                v.tensor_tensor(parts[:, w, 2, :], rf[:, w, :], parts[:, w, 1, :], ALU.subtract).then_inc(parts_done, 1)
            qk_chunks(v, rest)

            def maxima(u, chunks):
                for n in chunks:
                    i, kc, pr, hh = CHUNKS[n]
                    keys = min(512, (i + 1) * P - kc * 512)
                    v.wait_ge(max_mul, u * NP1 + (n + 1))
                    bank = ps[:, 5 + n % 2, 0:keys]
                    h = 2 * pr + hh
                    if kc == i // DIAG:
                        v.wait_ge(max_free, u * NP1 + (n + 1))
                        v.sem_inc(passed, 1)
                        v.tensor_tensor_reduce(out=junk[:, n % 2, 0:keys], in0=bank, in1=causal[:, 512 - keys:512], scale=1.0,
                                               scalar=LOWEST, op0=ALU.add, op1=ALU.max,
                                               accum_out=mx[:, h, i:i + 1]).then_inc(max_free, 1)
                    else:
                        v.tensor_reduce(mx0[:, h, i:i + 1], bank, AX_X, ALU.max).then_inc(max_free, 1)

            def join_maxima(u):
                v.wait_ge(max_free, (u + 1) * NP1 + 2)
                v.tensor_tensor(mx[:, :, DIAG:], mx[:, :, DIAG:], mx0[:, :, DIAG:], ALU.max).then_inc(max_done, 1)

            def split_maxima(u):
                v.wait_ge(max_put, u + 1)
                if not isinstance(u, int) or u > 0:
                    v.wait_ge(nm_out, u * DMA)
                v.tensor_scalar(nm[:, 0, :], ps[0:4 * QT, 7, 0:P], -1.0, None, ALU.mult).then_inc(misc_free, 1)
                v.wait_ge(misc_free, misc_number(u, "max") + 1)
                v.tensor_copy(nm_parts[:, 0, :], nm[:, 0, :]).then_inc(nm_dve, 1)
                v.wait_ge(nm_dve, u * 3 + 1)
                v.tensor_tensor(nm[:, 1, :], nm[:, 0, :], nm_parts[:, 0, :], ALU.subtract).then_inc(nm_dve, 1)
                v.wait_ge(nm_dve, u * 3 + 2)
                v.tensor_copy(nm_parts[:, 1, :], nm[:, 1, :]).then_inc(nm_dve, 1)
                v.wait_ge(nm_dve, u * 3 + 3)
                v.tensor_tensor(nm_parts[:, 2, :], nm[:, 1, :], nm_parts[:, 1, :], ALU.subtract).then_inc(nm_done, 1)

            def take_sums(u, c):
                v.wait_ge(prob_free, u * NSTEP + (PRING + (DIAG, NSTEP)[c]))
                v.wait_ge(yraw_free, u * NCH + (c + 1))
                v.tensor_copy(yraw[:, c, :], ps[:, 4, :]).then_inc(pv_free, 1)

            def divide(b, r, u, c, last):
                v.wait_ge(yraw_free, u * NCH + (NCH + c + 1))
                sums = ps[:, 7, :].rearrange("p (a h d) -> p a h d", a=DIAG, h=4)
                v.reciprocal(rden[:], sums[:, :, :, HD]).then_inc(rden_done, 1)
                v.wait_ge(rden_done, u * NCH + (c + 1))
                t0 = b * QT + DIAG * c
                v.tensor_tensor(z_sb[:, bass.ds(t0, DIAG), r * 4 * HD:(r + 1) * 4 * HD].rearrange("p a (h d) -> p a h d", h=4),
                                sums[:, :, :, 0:HD], rden[:].unsqueeze(3).broadcast_to([P, DIAG, 4, HD]), ALU.mult).then_inc(misc_free, 1)

            maxima(0, range(NP1))
            join_maxima(0)
            split_maxima(0)

            def quad(b, r, u, last):
                ahead = has(r, last, 1)
                for t in range(NSTEP):
                    if ahead and t < P1_STEPS:
                        maxima(u + 1, range(P1_PER * t, P1_PER * (t + 1)))
                    if t == DIAG - 1:
                        take_sums(u, 0)
                    if t == DIAG + 1:
                        divide(b, r, u, 0, last)
                    if ahead and t == P1_STEPS - 1:
                        join_maxima(u + 1)
                        split_maxima(u + 1)
                take_sums(u, 1)
                divide(b, r, u, 1, last)
            quads(v, quad)

            for g in range(NG):
                v.wait_ge(proj_mul, g + 1)
                xg = x_sb[:, G4 * g:G4 * (g + 1), :]
                v.tensor_tensor(xg, ps[:, 2 + g % 2, :].rearrange("p (a c) -> p a c", a=G4), xg, ALU.add).then_inc(proj_sum, 1)
                v.wait_ge(proj_sum, g + 1)
                v.tensor_tensor(xg, xg, bp_all[:].unsqueeze(1).broadcast_to([P, G4, C]), ALU.add).then_inc(att_added, 1)
            v.wait_ge(att_added, NG)

        def misc_number(u, what):
            return {"max": u * 3 - (0 if isinstance(u, int) and u == 0 else 1), "out0": u * 3 + 1, "out1": u * 3 + (2 if isinstance(u, int) and u == NQ - 1 else 3)}[what]

        def attention_pe_weights(pe):
            pe.wait_ge(small_in, SMALL_LOADS * DMA)
            pe.wait_ge(y_got, NS)
            for j in range(3):
                pe.transpose(ps[:, 6, j * P:(j + 1) * P], wattn_in[:, j, :], ident[:])
                pe.transpose(ps[0:R, 7, j * P:(j + 1) * P], lb_in[:, j, :], ident[:])
            pe.transpose(ps[:, 6, 3 * P:4 * P], wproj_in[:], ident[:])
            pe.transpose(ps[0:R, 7, 3 * P:4 * P], lbp_in[:], ident[:]).then_inc(wt_put, 1)
            pe.wait_ge(wt_got, 1)
            pe.matmul(ps[:, 6, 0:3 * C], la_in[:], lbT[:, 0:3 * C], start=True, stop=True)
            pe.matmul(ps[:, 6, 3 * C:], lap_in[:], lbT[:, 3 * C:], start=True, stop=True).then_inc(wt_put, 1)

        def attention_pe(pe):
            pe.wait_ge(wt_got, 2)
            pe.sem_inc(quad_free, 4)
            pe.sem_inc(max_free, 2)
            pe.sem_inc(pv_free, 1)
            pe.sem_inc(prob_free, PRING)
            pe.sem_inc(yraw_free, NCH)
            pe.wait_ge(zt_got, 2 * NG)
            for g in range(NG):
                if g >= 2:
                    pe.wait_ge(v_got, g - 1)
                for a in range(G4):
                    t = G4 * g + a
                    mm = pe.matmul(ps[:, 4 + g % 2, a * C:(a + 1) * C], zT[:, t * P:(t + 1) * P], w_all[:, 2 * C:3 * C], start=True, stop=True)
                mm.then_inc(v_mul, 1)

            def project(n, w, first):
                if not first:
                    pe.wait_ge(v32_got, n * 2 + (w - 1))
                pe.matmul(ps[:, 2 + w, :], w_all[:, w * C:(w + 1) * C], zT[:, bass.ds(n * CW, CW)], start=True, stop=True).then_inc(qk_put, 1)
            qk_chunks(pe, project)
            pe.wait_ge(v32_got, 2 * NQK)
            pe.wait_ge(v_got, NG)

            def max_scores(u, r, chunks):
                for n in chunks:
                    i, kc, pr, hh = CHUNKS[n]
                    keys = min(512, (i + 1) * P - kc * 512)
                    rows = slice(64 * hh, 64 * hh + SR)
                    pe.wait_ge(max_free, u * NP1 + (n + 1))
                    pe.matmul(ps[:, 5 + n % 2, 0:keys], q_stk[rows, r, pr, i * P:(i + 1) * P],
                              k_stk[rows, r, pr, kc * 512:kc * 512 + keys], start=True, stop=True).then_inc(max_mul, 1)

            def turn_maxima(u):
                pe.wait_ge(max_done, u + 1)
                if not isinstance(u, int) or u > 0:
                    pe.wait_ge(misc_free, misc_number(u, "max"))
                pe.transpose(ps[0:4 * QT, 7, 0:P], mx[:].rearrange("p h i -> p (h i)"), ident[:]).then_inc(max_put, 1)

            def scores(u, r, t):
                c, j = STEPS[t]
                n = width(t)
                if t == 0:
                    pe.wait_ge(nm_in, (u + 1) * 2 * DMA)
                for g in range(2):
                    if not (isinstance(u, int) and u == 0 and t == 0):
                        pe.wait_ge(exp_done[g], u * NSTEP + t)
                    for hh in range(2):
                        rows = slice(64 * hh, 64 * hh + KR)
                        mm = pe.matmul(ps[:, 2 * g + hh, 0:n], k_stk[rows, r, g, j * P:(j + 1) * P],
                                       q_stk[rows, r, g, (c + 1) * CW - n:(c + 1) * CW], start=True, stop=True)
                    mm.then_inc(score_mul[g], 1)

            def weigh(u, r, t):
                c, j = STEPS[t]
                n = width(t)
                for g in range(2):
                    pe.wait_ge(exp_done[g], u * NSTEP + (t + 1))
                if diag(t):
                    d = sum(diag(s) for s in range(t + 1))
                    pe.wait_ge(causal_done, u * 2 * NDIAG + 2 * d)
                if t == 0:
                    pe.wait_ge(vaug_in, u + 1)
                if j == 0:
                    pe.wait_ge(pv_free, u * NCH + (c + 1))
                for h in range(4):
                    mm = pe.matmul(ps[32 * h:32 * h + 32, 4, CW - n:CW], v_aug[:, r, j, h, :],
                                   prob[:, t % PRING, h // 2, h % 2, 0:n], start=(j == 0), stop=(j == DIAG * (c + 1) - 1))
                mm.then_inc(prob_free, 1)

            def turn_out(u, c):
                pe.wait_ge(pv_free, u * NCH + (c + 2))
                pe.wait_ge(misc_free, misc_number(u, f"out{c}"))
                for a in range(DIAG):
                    mm = pe.transpose(ps[:, 7, a * P:(a + 1) * P], yraw[:, c, a * P:(a + 1) * P], ident[:])
                    if c == NCH - 1 and a == 0:
                        mm.then_inc(quad_free, 1)
                mm.then_inc(yraw_free, 1)

            pe.wait_ge(stack_in[0], 4 * DMA)
            max_scores(0, 0, range(NP1))
            turn_maxima(0)
            scores(0, 0, 0)

            def quad(b, r, u, last):
                nxt = (r + 1) % QUADS
                ahead = has(r, last, 1)
                if ahead:
                    pe.wait_ge(stack_in[nxt], (b + ((r + 1) // QUADS + 1)) * 4 * DMA)
                for t in range(NSTEP):
                    if t + 1 < NSTEP:
                        scores(u, r, t + 1)
                    elif ahead:
                        scores(u + 1, nxt, 0)
                    if ahead and t < P1_STEPS:
                        max_scores(u + 1, nxt, range(P1_PER * t, P1_PER * (t + 1)))
                    weigh(u, r, t)
                    if t == DIAG:
                        turn_out(u, 0)
                    if ahead and t == P1_STEPS:
                        turn_maxima(u + 1)
                turn_out(u, 1)
            quads(pe, quad)

            def proj(g):
                pe.wait_ge(yt_got, g + 1)
                if g >= 2:
                    pe.wait_ge(proj_sum, g - 1)
                for a in range(G4):
                    t = G4 * g + a
                    mm = pe.matmul(ps[:, 2 + g % 2, a * C:(a + 1) * C], zT[:, t * P:(t + 1) * P], w_all[:, 3 * C:], start=True, stop=True)
                mm.then_inc(proj_mul, 1)
            pe.wait_ge(misc_free, misc_number(NQ - 1, "out1") + 1)
            for g in range(NG):
                if g >= 2:
                    pe.wait_ge(yt_got, g - 1)
                for a in range(G4):
                    mm = pe.transpose(ps[:, g % 2, a * P:(a + 1) * P], z_sb[:, G4 * g + a, :], ident[:])
                mm.then_inc(yt_put, 1)
                if g >= 1:
                    proj(g - 1)
            proj(NG - 1)

        def transposes(pe, n):
            for g in range(NG):
                pe.wait_ge(z_ready, NG * n + g + 1)
                if g >= 2:
                    pe.wait_ge(zt_got, NG * n + g - 1)
                for a in range(G4):
                    mm = pe.transpose(ps[:, g % 2, a * P:(a + 1) * P], z_sb[:, G4 * g + a, :], ident[:])
                mm.then_inc(zt_put, 1)
                yield g

        def take_transposes(act, n):
            for g in range(NG):
                act.wait_ge(zt_put, NG * n + g + 1)
                act.copy(zT[:, g * 512:(g + 1) * 512], ps[:, g % 2, :]).then_inc(zt_got, 1)

        @block.sync
        def _(sp):
            sp.dma_start(x_sb[:, 0:8, :], x_dram[:, 0:8, :]).then_inc(x_in[0], DMA)
            sp.dma_start(wg_in[:], wg).then_inc(gate_in, DMA)
            sp.dma_start(wgred_in[:], wg_red).then_inc(gate_in, DMA)
            for g in range(1, 4):
                sp.dma_start(x_sb[:, 8 * g:8 * g + 8, :], x_dram[:, 8 * g:8 * g + 8, :]).then_inc(x_in[g], DMA)
            sp.dma_start(bias_in[:, 0:BW1], b1.rearrange("e f -> (e f)").rearrange("(p n) -> p n", p=P)).then_inc(bias_i, DMA)
            sp.dma_start(bias_in[:, BW1:BF_W], b2.rearrange("e f -> (e f)").rearrange("(p n) -> p n", p=P)).then_inc(bias_i, DMA)
            sp.wait_ge(zeros_done, 1)
            sp.dma_start(slots.rearrange("(j p) c -> p j c", p=P), gath[:, 0:1, :].broadcast_to([P, NS, C])).then_inc(slots_clear, DMA)
            sp.dma_start(w1_sb[:], w1.rearrange("e c f -> c e f")).then_inc(w1_in, DMA)
            sp.dma_start(w2_sb[:], w2.rearrange("e (k p) c -> p e k c", p=P)).then_inc(w2_in, DMA)
            sp.wait_ge(bias_split, 1)
            for k in range(3):
                sp.dma_start(bias_d[k, 0:E * F].rearrange("(p n) -> p n", p=P), bias_parts[:, k, 0:BW1]).then_inc(bias_out, DMA)
                sp.dma_start(bias_d[k, E * F:].rearrange("(p n) -> p n", p=P), bias_parts[:, k, BW1:BF_W]).then_inc(bias_out, DMA)
            sp.wait_ge(bias_out, 6 * DMA)
            sp.wait_ge(consts, CONSTS)
            sp.dma_start(b1_rows[0:3, :], bias_d[:, 0:E * F]).then_inc(bias_back, DMA)
            sp.dma_start(b2_rows[0:3, :], bias_d[:, E * F:]).then_inc(bias_back, DMA)
            sp.dma_start(wattn_in[:], w_attn.rearrange("(j p) c -> p j c", p=P)).then_inc(small_in, DMA)
            sp.dma_start(la_in[:], la_attn).then_inc(small_in, DMA)
            sp.dma_start(lb_in[:], lb_attn.rearrange("(j p) r -> p j r", p=P)).then_inc(small_in, DMA)
            sp.dma_start(wproj_in[:], w_proj).then_inc(small_in, DMA)
            sp.dma_start(lap_in[:], la_proj).then_inc(small_in, DMA)
            sp.dma_start(lbp_in[:], lb_proj).then_inc(small_in, DMA)
            with nc.allow_non_contiguous_dma(reason="three bias values per partition"):
                sp.dma_start(b_qkv[:], b_attn.rearrange("(j p) -> p j", p=P)).then_inc(small_in, DMA)
            sp.dma_start(bv_all[:], b_attn[2 * C:].rearrange("(o c) -> o c", o=1).broadcast_to([P, C])).then_inc(small_in, DMA)
            sp.dma_start(bp_all[:], b_proj.rearrange("(o c) -> o c", o=1).broadcast_to([P, C])).then_inc(small_in, DMA)

            def moe(f):
                def step(s, r, turn):
                    if not runs(s, 0):
                        return
                    if later(s, 4):
                        sp.wait_ge(xt_put, s + (f * NS - 3))
                    sp.dma_start(xin[:, r, :], slots[bass.ds(s * P, P), :]).then_inc(slot_in[r], DMA)
                sp.wait_ge(scattered, (f + 1) * NT * DMA)
                tile_steps(sp, step)

            moe(0)
            attention_sp(sp)
            moe(1)
            for g in range(4):
                sp.wait_ge(moe_added, NT + 8 * (g + 1))
                sp.dma_start(out_dram[:, 8 * g:8 * g + 8, :], x_sb[:, 8 * g:8 * g + 8, :]).then_inc(out_done, DMA)
            sp.wait_ge(out_done, 4 * DMA)

        @block.gpsimd
        def _(pool):
            pool.memset(gath[:, 0, :], 0.0).then_inc(zeros_done, 1)
            pool.memset(ident[:], 0.0).then_inc(consts, 1)
            pool.memset(ones_bf[:], 1.0).then_inc(consts, 1)
            pool.memset(before[:], 1.0).then_inc(consts, 1)
            pool.memset(causal[:], 0.0).then_inc(consts, 1)
            pool.memset(scanA[:], 0.0).then_inc(consts, 1)
            pool.memset(scanB[:], 0.0).then_inc(consts, 1)
            pool.memset(padA[:], 0.0).then_inc(consts, 1)
            pool.memset(padB[:], 0.0).then_inc(consts, 1)
            pool.memset(b1_rows[:].bitcast(F32), 0.0).then_inc(consts, 1)
            pool.memset(b2_rows[:].bitcast(F32), 0.0).then_inc(consts, 1)
            pool.memset(minus_half[:], -0.5).then_inc(consts, 1)
            pool.iota(rev[:], [[-1, E]], base=E, channel_multiplier=0, allow_small_or_imprecise_dtypes=True).then_inc(consts, 1)
            pool.iota(starts[:], [[P, NS]], base=0, channel_multiplier=0, allow_small_or_imprecise_dtypes=True).then_inc(consts, 1)
            pool.wait_ge(consts, CONSTS - 3)
            pool.affine_select(out=ident[:], in_=ident[:], compare_op=ALU.not_equal, fill=1.0, base=0,
                               pattern=[[-1, P]], channel_multiplier=1).then_inc(consts, 1)
            pool.affine_select(out=before[:], in_=before[:], compare_op=ALU.is_gt, fill=0.0, base=0,
                               pattern=[[1, P]], channel_multiplier=-1).then_inc(consts, 1)
            pool.affine_select(out=causal[:, 384:512], in_=causal[:, 384:512], compare_op=ALU.is_ge, fill=LOWEST, base=0,
                               pattern=[[-1, P]], channel_multiplier=1).then_inc(consts, 1)

            def moe(f):
                pool.wait_ge(pos_done, f + 1)
                if f == 0:
                    pool.wait_ge(slots_clear, DMA)
                for a in range(NT):
                    pool.indirect_dma_start(
                        out=slots, out_offset=bass.IndirectOffsetOnAxis(ap=pos[:, a:a + 1].bitcast(U32), axis=0),
                        in_=z_sb[:, a, :], in_offset=None, bounds_check=NS * P - 1).then_inc(scattered, DMA)
                for r in range(4):
                    pool.wait_ge(y_out[r], (f + 1) * per_ring(r) * DMA)
                for a in range(NT):
                    pool.indirect_dma_start(
                        out=gath[:, a, :], out_offset=None, in_=yslots,
                        in_offset=bass.IndirectOffsetOnAxis(ap=pos[:, a:a + 1].bitcast(U32), axis=0),
                        bounds_check=NS * P - 1).then_inc(gathered[a // 8], DMA)

            def deviation(n):
                pool.wait_ge(root_in, n + 2)
                pool.tensor_tensor(rstd[:], lnw[:, 5, :], minus_half[:], ALU.pow).then_inc(root_done, 1)

            pool.wait_ge(root_in, 1)
            pool.tensor_tensor(wg_n[:, 1:2], wg_n[:, 0:1], minus_half[0:E, 0:1], ALU.pow).then_inc(root_done, 1)
            deviation(0)
            moe(0)
            deviation(1)
            attention_pool(pool)
            deviation(2)
            moe(1)

        @block.vector
        def _(v):
            n_dve = [0]

            def put(ins):
                n_dve[0] += 1
                ins.then_inc(dve, 1)

            def own():
                v.wait_ge(dve, n_dve[0])

            def square_gate():
                v.wait_ge(gate_in, 2 * DMA)
                v.tensor_tensor_reduce(out=wg_sq[:], in0=wg_in[:], in1=wg_in[:], scale=1.0, scalar=0.0,
                                       op0=ALU.mult, op1=ALU.add, accum_out=wg_n[:, 0:1]).then_inc(root_in, 1)

            def prepare():
                v.wait_ge(root_done, 1)
                put(v.tensor_scalar(wg_n[:, 2:3], wg_n[:, 1:2], 1.0 / NORM_EPS, None, ALU.min))
                own()
                v.tensor_scalar(wg_unit[:], wg_in[:], wg_n[:, 2:3], None, ALU.mult).then_inc(gate_sub, 1)
                v.wait_ge(bias_i, 2 * DMA)
                put(v.tensor_copy(bias_parts[:, 0, :], bias_in[:]))
                own()
                put(v.tensor_tensor(bias_r[:, 0, :], bias_in[:], bias_parts[:, 0, :], ALU.subtract))
                own()
                put(v.tensor_copy(bias_parts[:, 1, :], bias_r[:, 0, :]))
                own()
                v.tensor_tensor(bias_parts[:, 2, :], bias_r[:, 0, :], bias_parts[:, 1, :], ALU.subtract).then_inc(bias_split, 1)
                v.wait_ge(wprep_pe, 1)
                v.tensor_copy(wgT[:], ps[0:GD, 2, 0:E]).then_inc(wprep_got, 1)
                v.wait_ge(wprep_pe, 2)
                v.tensor_copy(wgate[:], ps[:, 2, 0:E]).then_inc(wprep_got, 1)

            def layer_norm(n):
                with v.Fori(0, NG) as g:
                    for a in range(G4):
                        last = v.bn_stats(stats[:, bass.ds(g * G4 + a, 1), :].rearrange("p a c -> p (a c)"),
                                          x_sb[:, bass.ds(g * G4 + a, 1), :].rearrange("p a c -> p (a c)"))
                    last.then_inc(bn_done, 1)
                v.wait_ge(bn_done, NG * (n + 1))
                me, mo, qe, qo = (stats[:, :, k] for k in (1, 4, 2, 5))
                put(v.tensor_tensor(lnw[:, 0, :], me, mo, ALU.add))
                put(v.tensor_tensor(lnw[:, 1, :], me, mo, ALU.subtract))
                put(v.tensor_tensor(lnw[:, 2, :], qe, qo, ALU.add))
                own()
                put(v.tensor_scalar(mean[:], lnw[:, 0, :], 0.5, None, ALU.mult))
                put(v.tensor_tensor(lnw[:, 3, :], lnw[:, 1, :], lnw[:, 1, :], ALU.mult))
                put(v.tensor_scalar(lnw[:, 4, :], lnw[:, 2, :], 1.0 / C, LN_EPS, ALU.mult, ALU.add))
                own()
                v.scalar_tensor_tensor(out=lnw[:, 5, :], in0=lnw[:, 3, :], scalar=0.25, in1=lnw[:, 4, :],
                                       op0=ALU.mult, op1=ALU.add).then_inc(root_in, 1)
                v.wait_ge(root_done, n + 2)
                with v.Fori(0, NG) as g:
                    for a in range(G4):
                        t = g * G4 + a
                        last = v.tensor_scalar(z_sb[:, bass.ds(t, 1), :].rearrange("p a c -> p (a c)"),
                                               x_sb[:, bass.ds(t, 1), :].rearrange("p a c -> p (a c)"),
                                               mean[:, bass.ds(t, 1)], rstd[:, bass.ds(t, 1)], ALU.subtract, ALU.mult)
                    last.then_inc(z_ready, 1)

            def over_e(t):
                return t.unsqueeze(2).broadcast_to([P, NT, E])

            def route(f):
                v.wait_ge(logits_done, f + 1)
                put(v.tensor_copy(logit[:], ps[:, 7, 0:NT * E].rearrange("p (a e) -> p a e", e=E)))
                own()
                put(v.tensor_reduce(gmax[:, 0, :], logit[:], AX_X, ALU.max))
                own()
                v.tensor_tensor(gtmp[:], logit[:], over_e(gmax[:, 0, :]), ALU.subtract).then_inc(gate_sub, 1)
                put(v.tensor_tensor(logit[:], logit[:], over_e(gmax[:, 0, :]), ALU.is_equal))
                own()
                put(v.tensor_tensor(logit[:], logit[:], rev[:].unsqueeze(1).broadcast_to([P, NT, E]), ALU.mult))
                own()
                put(v.tensor_reduce(gmax[:, 1, :], logit[:], AX_X, ALU.max))
                own()
                v.tensor_tensor(onehot[:], logit[:], over_e(gmax[:, 1, :]), ALU.is_equal).then_inc(onehot_done, 1)
                v.wait_ge(gate_exp, f + 1)
                put(v.tensor_reduce(gmax[:, 2, :], gexp[:], AX_X, ALU.add))
                own()
                put(v.reciprocal(score[:], gmax[:, 2, :]))
                own()
                put(v.tensor_scalar(score[:], score[:], BRANCH, None, ALU.mult))
                v.wait_ge(counted, f + 1)
                H = NT // 2
                tot = ps[:, 6, NT * E:2 * NT * E].rearrange("p (a e) -> p a e", e=E)
                front = ps[:, 6, 0:NT * E].rearrange("p (a e) -> p a e", e=E)
                put(v.tensor_copy(scanA[:, H:, :], tot))
                own()
                src, dst, d = scanA, scanB, 1
                while d < NT:
                    put(v.tensor_tensor(dst[:, H:, :], src[:, H:, :], src[:, H - d:H + NT - d, :], ALU.add))
                    own()
                    src, dst, d = dst, src, 2 * d
                put(v.tensor_scalar(cnt_i[:, 0, :], src[:, H + NT - 1, :], float(P - 1), None, ALU.add))
                own()
                SH = P.bit_length() - 1
                put(v.tensor_scalar(cnt_i[:, 1, :], cnt_i[:, 0, :], SH, SH, ALU.logical_shift_right, ALU.logical_shift_left))
                own()
                put(v.tensor_copy(padA[:, E // 2:], cnt_i[:, 1, :]))
                own()
                put(v.tensor_scalar(ebase[:], padA[:, E // 2:], -1.0, None, ALU.mult))
                a, b, d = padA, padB, 1
                while d < E:
                    put(v.tensor_tensor(b[:, E // 2:], a[:, E // 2:], a[:, E // 2 - d:E // 2 + E - d], ALU.add))
                    own()
                    a, b, d = b, a, 2 * d
                ends = a[:, E // 2:]
                put(v.tensor_tensor(ebase[:], ebase[:], ends, ALU.add))
                put(v.tensor_tensor(slot_of[:], src[:, H:, :], tot, ALU.subtract))
                own()
                put(v.tensor_tensor(slot_of[:], slot_of[:], front, ALU.add))
                own()
                put(v.tensor_tensor(slot_of[:], slot_of[:], ebase[:].unsqueeze(1).broadcast_to([P, NT, E]), ALU.add))
                own()
                put(v.tensor_tensor(slot_of[:], slot_of[:], onehot[:], ALU.mult))
                own()
                put(v.tensor_reduce(pos_f[:], slot_of[:], AX_X, ALU.add))
                own()
                v.tensor_copy(pos[:], pos_f[:]).then_inc(pos_done, 1)
                put(v.tensor_tensor(ecmp[:], starts[:].unsqueeze(2).broadcast_to([1, NS, E - 1]),
                                    ends[0:1, 0:E - 1].unsqueeze(1).broadcast_to([1, NS, E - 1]), ALU.is_ge))
                own()
                put(v.tensor_reduce(etab_f[:], ecmp[:], AX_X, ALU.add))
                own()
                v.tensor_copy(etab[:], etab_f[:]).then_inc(etab_done, 1)

            def experts(f):
                base = f * NS

                def step(s, r, turn):
                    if runs(s, 0):
                        v.wait_ge(xt_put, s + (base + 1))
                        if later(s, 2):
                            v.wait_ge(up_done, s + (base - 1))
                        v.tensor_copy(xs[:, r % 2, :], ps[:, r % 2, 0:P]).then_inc(xt_got, 1)
                    if runs(s, 2):
                        v.wait_ge(ht_put, s + (base - 1))
                        if later(s, 4):
                            v.wait_ge(down_done, s + (base - 3))
                        v.tensor_copy(hT[:, r % 2, :, :], ps[:, 4 + r % 2, :].rearrange("p (k c) -> p k c", k=FK)).then_inc(ht_got, 1)

                tile_steps(v, step)
                for g in range(4):
                    v.wait_ge(gathered[g], (f + 1) * 8 * DMA)
                    for a in range(8 * g, 8 * g + 8):
                        v.scalar_tensor_tensor(out=x_sb[:, a, :], in0=gath[:, a, :], scalar=score[:, a:a + 1],
                                               in1=x_sb[:, a, :], op0=ALU.mult, op1=ALU.add).then_inc(moe_added, 1)

            v.wait_ge(consts, CONSTS)
            square_gate()
            for g in range(4):
                v.wait_ge(x_in[g], DMA)
            layer_norm(0)
            prepare()
            route(0)
            experts(0)
            v.wait_ge(moe_added, NT)
            prepare_attention(v, put, own)
            layer_norm(1)
            attention_dve(v)
            layer_norm(2)
            route(1)
            experts(1)

        @block.scalar
        def _(act):
            def gate(f):
                act.wait_ge(gate_sub, f + 2)
                act.activation(gexp[:], gtmp[:], ACT.Exp).then_inc(gate_exp, 1)

            def experts(f):
                base = f * NS

                def step(s, r, turn):
                    if runs(s, 1):
                        act.wait_ge(up_done, s + base)
                        if later(s, 3):
                            act.wait_ge(ht_put, s + (base - 2))
                        act.activation(hid[:, (r - 1) % 2, :], ps[:, 2 + (r - 1) % 2, :], ACT.Gelu).then_inc(gelu_done, 1)
                    if runs(s, 3):
                        act.wait_ge(down_done, s + (base - 2))
                        q = (r - 3) % 4
                        full = turn if r == 3 else turn - 1
                        if not isinstance(full, int) or full > 0:
                            act.wait_ge(y_out[q], (full + f * per_ring(q)) * DMA)
                        act.copy(yr[:, q, :], ps[:, 6 + (r - 3) % 2, 0:C]).then_inc(y_got, 1)
                        act.wait_ge(y_got, s + (base - 2))
                        act.dma_start(yslots[bass.ds((s - 3) * P, P), :], yr[:, q, :]).then_inc(y_out[q], DMA)

                tile_steps(act, step)

            take_transposes(act, 0)
            gate(0)
            experts(0)
            take_transposes(act, 1)
            attention_act(act)
            take_transposes(act, 2)
            gate(1)
            experts(1)

        @block.tensor
        def _(pe):
            def prepare():
                pe.wait_ge(consts, CONSTS)
                pe.wait_ge(gate_sub, 1)
                pe.transpose(ps[0:GD, 2, 0:E], wg_unit[:], ident[0:E, 0:E]).then_inc(wprep_pe, 1)
                pe.wait_ge(wprep_got, 1)
                pe.matmul(ps[:, 2, 0:E], wgred_in[:], wgT[:], start=True, stop=True).then_inc(wprep_pe, 1)
                pe.wait_ge(wprep_got, 2)

            def gate(f, n):
                def logits(g):
                    pe.wait_ge(zt_got, NG * n + g + 1)
                    for a in range(G4 * g, G4 * g + G4):
                        mm = pe.matmul(ps[:, 7, a * E:(a + 1) * E], zT[:, a * P:(a + 1) * P], wgate[:], start=True, stop=True)
                    return mm
                for g in transposes(pe, n):
                    if g >= 1:
                        logits(g - 1)
                logits(NG - 1).then_inc(logits_done, 1)
                pe.wait_ge(onehot_done, f + 1)
                oh = onehot[:].rearrange("p a e -> p (a e)")
                pe.matmul(ps[:, 6, 0:NT * E], before[:], oh, start=True, stop=True)
                pe.matmul(ps[:, 6, NT * E:2 * NT * E], ones_bf[:], oh, start=True, stop=True).then_inc(counted, 1)

            def experts(f):
                base = f * NS
                pe.wait_ge(etab_done, f + 1)
                if f == 0:
                    pe.wait_ge(w1_in, DMA)
                    pe.wait_ge(w2_in, DMA)
                    pe.wait_ge(bias_back, 2 * DMA)

                def step(s, r, turn):
                    if runs(s, 0):
                        pe.wait_ge(slot_in[r], (turn + (f * per_ring(r) + 1)) * DMA)
                        if later(s, 2):
                            pe.wait_ge(xt_got, s + (base - 1))
                        pe.transpose(ps[:, r % 2, 0:P], xin[:, r, :], ident[:]).then_inc(xt_put, 1)
                    if runs(s, 1):
                        b = 2 + (r - 1) % 2
                        e = pe.value_load(etab[0:1, bass.ds(s - 1, 1)], min_val=0, max_val=E - 1)
                        pe.wait_ge(xt_got, s + base)
                        if later(s, 3):
                            pe.wait_ge(gelu_done, s + (base - 2))
                        pe.matmul(ps[:, b, :], xs[:, (r - 1) % 2, :], w1_sb[:, bass.ds(e, 1), :].rearrange("p e f -> p (e f)"),
                                  start=True, stop=False)
                        pe.matmul(ps[:, b, :], ones_bf[:], b1_rows[:, bass.ds(e * F, F)], start=False, stop=True).then_inc(up_done, 1)
                    if runs(s, 2):
                        b = 4 + r % 2
                        pe.wait_ge(gelu_done, s + (base - 1))
                        if later(s, 4):
                            pe.wait_ge(ht_got, s + (base - 3))
                        for k in range(FK):
                            mm = pe.transpose(ps[:, b, k * P:(k + 1) * P], hid[:, r % 2, k * P:(k + 1) * P], ident[:])
                        mm.then_inc(ht_put, 1)
                    if runs(s, 3):
                        b = 6 + (r - 3) % 2
                        e = pe.value_load(etab[0:1, bass.ds(s - 3, 1)], min_val=0, max_val=E - 1)
                        pe.wait_ge(ht_got, s + (base - 2))
                        if later(s, 5):
                            pe.wait_ge(y_got, s + (base - 4))
                        for k in range(FK):
                            pe.matmul(ps[:, b, 0:C], hT[:, (r - 3) % 2, k, :], w2_sb[:, bass.ds(e, 1), k, :].rearrange("p e c -> p (e c)"),
                                      start=(k == 0), stop=False)
                        pe.matmul(ps[:, b, 0:C], ones_bf[:], b2_rows[:, bass.ds(e * C, C)], start=False, stop=True).then_inc(down_done, 1)

                tile_steps(pe, step)

            prepare()
            gate(0, 0)
            experts(0)
            attention_pe_weights(pe)
            for _ in transposes(pe, 1):
                pass
            attention_pe(pe)
            gate(1, 2)
            experts(1)


_INS = ['L0_attn_x', 'L0_attn_w_attn', 'L0_attn_b_attn', 'L0_attn_la_attn', 'L0_attn_lb_attn', 'L0_attn_w_proj',
        'L0_attn_b_proj', 'L0_attn_la_proj', 'L0_attn_lb_proj', 'L0_ffn_wg_red', 'L0_ffn_wg', 'L0_ffn_w1',
        'L0_ffn_b1', 'L0_ffn_w2', 'L0_ffn_b2']


def kernel(**inputs):
    import numpy as _np
    import concourse.bacc as _bacc
    from concourse import mybir as _mybir
    from concourse.bass_utils import run_bass_kernel_spmd as _run

    nc = _bacc.Bacc("TRN2", target_bir_lowering=False, num_devices=1)
    arrays, args = {}, []
    for name in _INS:
        a = _np.ascontiguousarray(inputs[name])
        arrays[f"in_{name}_dram"] = a
        args.append(nc.dram_tensor(f"in_{name}_dram", a.shape, _mybir.dt.from_np(a.dtype), kind="ExternalInput").ap())
    shape = inputs["L0_attn_x"].shape
    args.append(nc.dram_tensor("out_0_dram", shape, _mybir.dt.float32, kind="ExternalOutput").ap())
    macaron_kernel(nc, *args)
    r = _run(nc, [arrays], core_ids=[0])
    return r.results[0]["out_0_dram"]
```

```python
from contextlib import ExitStack

import concourse.bass as bass
from concourse import mybir

P = 128
ALU = mybir.AluOpType
ACT = mybir.ActivationFunctionType
F32 = mybir.dt.float32
BF16 = mybir.dt.bfloat16
I32 = mybir.dt.int32
U32 = mybir.dt.uint32
AX_X = mybir.AxisListType.X

LN_EPS = 1e-5
NORM_EPS = 1e-4
LORA_SCALE = 0.5
BRANCH = 0.5
LOWEST = -3.0e38
HEADS = 16
G4 = 4
DMA = 16

Q_PARTS = (0, 0, 0, 1, 1, 2, 1)
K_PARTS = (0, 1, 2, 0, 1, 0, 2)


def macaron_kernel(nc, x, w_attn, b_attn, la_attn, lb_attn, w_proj, b_proj, la_proj, lb_proj,
                   wg_red, wg, w1, b1, w2, b2, out):
    B, T, C = x.shape
    N = B * T
    NT = N // P
    NG = NT // G4
    E, _, F = w1.shape
    FK = F // P
    GD = wg.shape[1]
    R = la_attn.shape[0]
    NS = NT + E - 1
    HD = C // HEADS
    SCALE = float(HD) ** -0.5
    QUADS = HEADS // 4
    QT = T // P
    CW = 512
    NCH = T // CW
    DIAG = CW // P
    SR = len(Q_PARTS) * HD
    KR = SR + 3
    STEPS = [(c, j) for c in range(NCH) for j in range(DIAG * (c + 1))]
    NSTEP = len(STEPS)
    CHUNKS = [(i, kc, pr, hh) for i in range(QT) for kc in range(i // DIAG + 1) for pr in range(2) for hh in range(2)]
    NP1 = len(CHUNKS)
    MAX_PER = NP1 // NSTEP
    MAX_LEAD = 6
    MAX_ITEMS = NP1 + 1
    NQ = B * QUADS
    PRING = 3
    assert C == P and NP1 % NSTEP == 0 and NSTEP % PRING == 0 and NT % 8 == 0
    assert MAX_PER == 4 and MAX_LEAD % 2 == 0 and DIAG % 2 == 0

    def diag(t):
        c, j = STEPS[t]
        return j >= DIAG * c

    def width(t):
        c, j = STEPS[t]
        return CW - P * max(0, j - DIAG * c)

    NDIAG = sum(diag(t) for t in range(NSTEP))

    with ExitStack() as ctx:
        def sb(name, shape, dt):
            return ctx.enter_context(nc.sbuf_tensor(name, shape, dt))

        def sem(name):
            return ctx.enter_context(nc.semaphore(name))

        def dram(name, shape, dt):
            return nc.dram_tensor(name, shape, dt, kind="Internal").ap()

        ps = ctx.enter_context(nc.psum_tensor("ps", [P, 8, 512], F32))

        x_sb = sb("x_sb", [P, NT, C], F32)
        z_sb = sb("z_sb", [P, NT, C], F32)
        zT = sb("zT", [P, N], F32)
        w1_sb = sb("w1_sb", [P, E, F], F32)
        w2_sb = sb("w2_sb", [P, E, FK, C], F32)
        b1_rows = sb("b1_rows", [P, E * F], BF16)
        b2_rows = sb("b2_rows", [P, E * C], BF16)
        w_all = sb("w_all", [P, 4 * C], F32)
        wgate = sb("wgate", [P, E], F32)
        b_qkv = sb("b_qkv", [P, 3], F32)
        bv_all = sb("bv_all", [P, C], F32)
        bp_all = sb("bp_all", [P, C], F32)

        ident = sb("ident", [P, P], F32)
        ones_bf = sb("ones_bf", [P, P], BF16)
        before = sb("before", [P, P], BF16)
        causal = sb("causal", [P, 512], F32)
        rev = sb("rev", [P, E], F32)
        minus_half = sb("minus_half", [P, NT], F32)
        starts = sb("starts", [1, NS], F32)

        stats = sb("stats", [P, NT, 6], F32)
        lnw = sb("lnw", [P, 6, NT], F32)
        mean = sb("mean", [P, NT], F32)
        rstd = sb("rstd", [P, NT], F32)
        logit = sb("logit", [P, NT, E], F32)
        gtmp = sb("gtmp", [P, NT, E], F32)
        slot_of = sb("slot_of", [P, NT, E], F32)
        gexp = sb("gexp", [P, NT, E], F32)
        gmax = sb("gmax", [P, 3, NT], F32)
        score = sb("score", [P, NT], F32)
        onehot = sb("onehot", [P, NT, E], BF16)
        scanA = sb("scanA", [P, NT // 2 + NT, E], F32)
        scanB = sb("scanB", [P, NT // 2 + NT, E], F32)
        cnt_i = sb("cnt_i", [P, 2, E], I32)
        padA = sb("padA", [P, E // 2 + E], F32)
        padB = sb("padB", [P, E // 2 + E], F32)
        ebase = sb("ebase", [P, E], F32)
        pos_f = sb("pos_f", [P, NT], F32)
        pos = sb("pos", [P, NT], I32)
        ecmp = sb("ecmp", [1, NS, E - 1], F32)
        etab_f = sb("etab_f", [1, NS], F32)
        etab = sb("etab", [1, NS], I32)

        AW = 2 * (4 * 2 * T // 2) + 4 * QT * P + PRING * 4 * CW
        arena = sb("arena", [P, AW], F32)

        def carve(at, words):
            assert at + words <= AW
            return arena[:, at:at + words], at + words

        gath, at = carve(0, NT * C)
        xin, at = carve(at, 4 * C)
        xs, at = carve(at, 2 * P)
        hid, at = carve(at, 2 * F)
        hT, at = carve(at, 2 * F)
        yr, at = carve(at, 4 * C)
        gath = gath.rearrange("p (a c) -> p a c", a=NT)
        xin = xin.rearrange("p (r c) -> p r c", r=4)
        xs = xs.rearrange("p (r c) -> p r c", r=2)
        hid = hid.rearrange("p (r c) -> p r c", r=2)
        hT = hT.rearrange("p (r k c) -> p r k c", r=2, k=FK)
        yr = yr.rearrange("p (r c) -> p r c", r=4)

        q_stk, at = carve(0, 4 * 2 * T // 2)
        k_stk, at = carve(at, 4 * 2 * T // 2)
        v_aug, at = carve(at, 4 * QT * P)
        prob, _ = carve(at, PRING * 4 * CW)
        vf, at = carve(at, 2 * CW)
        rf, at = carve(at, 2 * CW)
        parts, at = carve(at, 3 * CW)
        q_stk = q_stk.bitcast(BF16).rearrange("p (s r t) -> p s r t", s=4, r=2)
        k_stk = k_stk.bitcast(BF16).rearrange("p (s r t) -> p s r t", s=4, r=2)
        v_aug = v_aug.rearrange("p (s j h d) -> p s j h d", s=4, j=QT, h=4)
        prob = prob.rearrange("p (s g h n) -> p s g h n", s=PRING, g=2, h=2)
        vf = vf.rearrange("p (r n) -> p r n", r=2)
        rf = rf.rearrange("p (r n) -> p r n", r=2)
        parts = parts.bitcast(BF16).rearrange("p (r s n) -> p r s n", r=2, s=3)

        v_all = sb("v_all", [P, NT, C], F32)
        yraw = sb("yraw", [P, NCH, CW], F32)
        rden = sb("rden", [P, NCH, DIAG, 4], F32)
        junk = sb("junk", [P, 2, 512], BF16)
        mx = sb("mx", [P, 2, 4, QT], F32)
        mx0 = sb("mx0", [P, 4, QT], F32)
        nm = sb("nm", [4 * QT, 3, P], F32)
        nm_parts = sb("nm_parts", [4 * QT, 3, P], BF16)

        wattn_in, at = carve(at, 3 * C)
        la_in, at = carve(at, C)
        lb_in, at = carve(at, 3 * R)
        wproj_in, at = carve(at, C)
        lap_in, at = carve(at, C)
        lbp_in, at = carve(at, R)
        lbT, at = carve(at, 4 * C)
        wattn_in = wattn_in.rearrange("p (j c) -> p j c", j=3)
        lb_in = lb_in.rearrange("p (j r) -> p j r", j=3)
        la_in, lap_in, lbT = la_in[0:R], lap_in[0:R], lbT[0:R]
        wgred_in = sb("wgred_in", [GD, C], F32)
        wg_in = sb("wg_in", [E, GD], F32)
        wg_sq = sb("wg_sq", [E, GD], F32)
        wg_n = sb("wg_n", [E, 3], F32)
        wg_unit = sb("wg_unit", [E, GD], F32)
        wgT = sb("wgT", [GD, E], F32)
        BF_W = E * (F + C) // P
        bias_in = sb("bias_in", [P, BF_W], F32)
        bias_r = sb("bias_r", [P, 2, BF_W], F32)
        bias_parts = sb("bias_parts", [P, 3, BF_W], BF16)

        slots = dram("slots", [NS * P, C], F32)
        yslots = dram("yslots", [NS * P, C], F32)
        bias_d = dram("bias_d", [3, E * (F + C)], BF16)
        stack_d = dram("stack_d", [2, HEADS, SR, N], BF16)
        nm_d = dram("nm_d", [3, 4 * QT, P], BF16)
        x_dram = x.rearrange("b t c -> (b t) c").rearrange("(a p) c -> p a c", p=P)
        out_dram = out.rearrange("b t c -> (b t) c").rearrange("(a p) c -> p a c", p=P)
        BW1 = E * F // P

        block = ctx.enter_context(nc.Block())
        TILE_STEPS = NS + 3
        FIRST = 8
        LAST = FIRST + 4 * ((NS - FIRST) // 4)

        def tile_steps(eng, step):
            for s in range(FIRST):
                step(s, s % 4, s // 4)
            with eng.Fori(FIRST // 4, LAST // 4) as turn:
                for r in range(4):
                    step(turn * 4 + r, r, turn)
            for s in range(LAST, TILE_STEPS):
                step(s, s % 4, s // 4)

        def runs(s, lag):
            return not isinstance(s, int) or 0 <= s - lag < NS

        def later(s, lag):
            return not isinstance(s, int) or s - lag >= 0

        def per_ring(r):
            return (NS - r + 3) // 4

        x_in = [sem(f"x_in{g}") for g in range(4)]
        w1_in, w2_in, small_in, gate_in, bias_i, bias_out, bias_back = (
            sem(n) for n in ("w1_in", "w2_in", "small_in", "gate_in", "bias_i", "bias_out", "bias_back"))
        consts, zeros_done, slots_clear = sem("consts"), sem("zeros_done"), sem("slots_clear")
        CONSTS = 16
        bn_done, etab_done, root_in, root_done = sem("bn_done"), sem("etab_done"), sem("root_in"), sem("root_done")
        dve = sem("dve")
        wprep_pe, wprep_got = sem("wprep_pe"), sem("wprep_got")
        bias_split = sem("bias_split")
        z_ready, zt_put, zt_got = sem("z_ready"), sem("zt_put"), sem("zt_got")
        logits_done, gate_sub, gate_exp, onehot_done, counted, pos_done = (
            sem(n) for n in ("logits_done", "gate_sub", "gate_exp", "onehot_done", "counted", "pos_done"))
        scattered = sem("scattered")
        slot_in = [sem(f"slot_in{r}") for r in range(4)]
        xt_put, xt_got, up_done, gelu_done, ht_put, ht_got, down_done, y_got = (
            sem(n) for n in ("xt_put", "xt_got", "up_done", "gelu_done", "ht_put", "ht_got", "down_done", "y_got"))
        y_out = [sem(f"y_out{r}") for r in range(4)]
        gathered = [sem(f"gathered{g}") for g in range(4)]
        moe_added, out_done = sem("moe_added"), sem("out_done")

        SMALL_LOADS = 9
        wt_put, wt_got = sem("wt_put"), sem("wt_got")
        qk_put, v32_got, hi_got, rest_got, mid_got, parts_done = (
            sem(n) for n in ("qk_put", "v32_got", "hi_got", "rest_got", "mid_got", "parts_done"))
        qk_out = [sem("q_out"), sem("k_out")]
        v_mul, v_got, k_ones, v_ones = sem("v_mul"), sem("v_got"), sem("k_ones"), sem("v_ones")
        stack_in = [sem(f"stack_in{s}") for s in range(4)]
        quad_free, vaug_in = sem("quad_free"), sem("vaug_in")
        max_mul, max_free, max_done = sem("max_mul"), sem("max_free"), sem("max_done")
        nm_pool, nm_done, nm_out, nm_in = sem("nm_pool"), sem("nm_done"), sem("nm_out"), sem("nm_in")
        score_mul = [sem("score_mulA"), sem("score_mulB")]
        exp_done = [sem("exp_doneA"), sem("exp_doneB")]
        causal_done, prob_free, sums_got, turned, rden_done = (
            sem(n) for n in ("causal_done", "prob_free", "sums_got", "turned", "rden_done"))
        pv_free = [sem(f"pv_free{c}") for c in range(NCH)]
        y_ready, yt_put, yt_got, proj_mul, proj_sum, att_added = (
            sem(n) for n in ("y_ready", "yt_put", "yt_got", "proj_mul", "proj_sum", "att_added"))
        passed, passed_pool = sem("passed"), sem("passed_pool")
        OUT_RUN = len(Q_PARTS) * DMA
        NQK = N // CW

        def quads(eng, quad):
            with eng.Fori(0, B - 1) as b:
                for r in range(QUADS):
                    quad(b, r, b * QUADS + r)
            for r in range(QUADS):
                quad(B - 1, r, (B - 1) * QUADS + r)

        BATCH_STEPS = QUADS * NSTEP

        def score_steps(eng, step, head, tail):
            def at(b, g):
                q, t = divmod(g, NSTEP)
                step(b, q, b * QUADS + q, t)
            for g in range(head):
                at(0, g)
            with eng.Fori(0, B - 1) as b:
                for g in range(head, head + BATCH_STEPS):
                    at(b, g)
            for g in range(head, BATCH_STEPS + tail):
                at(B - 1, g)

        def real(u):
            return not isinstance(u, int) or 0 <= u < NQ

        def max_chunks(t):
            n = MAX_PER * (t + MAX_LEAD)
            ahead, n = (1, n) if n < NP1 else (2, n - NP1)
            return ahead, range(n, n + MAX_PER)

        def first(u):
            return isinstance(u, int) and u == 0

        def chunk_item(u, n):
            return n if first(u) else u * MAX_ITEMS + (n - 1 + (n >= MAX_PER))

        def turn_item(u):
            return (u + 1) * MAX_ITEMS + (MAX_PER - 1 if real(u + 1) else -1)

        def chunk_bank(u, r, n):
            return 5 + (n if first(u) else r * MAX_ITEMS + n - 1 + (n >= MAX_PER)) % 2

        def turn_bank(u, r):
            return 5 + ((r + 1) * MAX_ITEMS + (MAX_PER if real(u + 1) else 0) - 1) % 2

        PV_BANK = (4, 7)

        def qk_chunks(eng, chunk):
            for w in range(2):
                chunk(0, w, True)
            with eng.Fori(1, NQK) as n:
                for w in range(2):
                    chunk(n, w, False)

        def attention_sp(sp):
            def store(n, w, first):
                sp.wait_ge(parts_done, n * 2 + (w + 1))
                for k in range(len(Q_PARTS)):
                    part = (Q_PARTS, K_PARTS)[w][k]
                    sp.dma_start(stack_d[w, :, HD * k:HD * (k + 1), bass.ds(n * CW, CW)], parts[:, w, part, :]).then_inc(qk_out[w], DMA)

            qk_chunks(sp, store)
            for w in range(2):
                sp.wait_ge(qk_out[w], NQK * OUT_RUN)
            sp.wait_ge(k_ones, 1)

            def load_stack(b, r, u):
                sp.wait_ge(quad_free, u + 1)
                for w, stk in ((0, q_stk), (1, k_stk)):
                    for half in range(2):
                        src = stack_d[w, 4 * r + half:4 * r + half + 3:2, :, bass.ds(b * T, T)].rearrange("h s t -> s h t")
                        sp.dma_start(stk[64 * half:64 * half + SR, r, :, :], src).then_inc(stack_in[r], DMA)

            def pass_maxima(r, u):
                sp.wait_ge(nm_done, u + 1)
                if not isinstance(u, int) or u > 0:
                    sp.wait_ge(nm_in, u * 2 * DMA)
                sp.dma_start(nm_d.rearrange("s m q -> m s q"), nm_parts[:]).then_inc(nm_out, DMA)
                sp.wait_ge(nm_out, (u + 1) * DMA)
                rows = nm_d.rearrange("s (g h i) q -> h s g (i q)", g=2, h=2)
                for half in range(2):
                    sp.dma_start(q_stk[64 * half + SR:64 * half + KR, r, :, :], rows[half]).then_inc(nm_in, DMA)

            load_stack(0, 0, 0)
            load_stack(0, 1, 1)
            pass_maxima(0, 0)

            def quad(b, r, u):
                if real(u + 2):
                    load_stack(b + (r + 2) // QUADS, (r + 2) % QUADS, u + 2)
                if real(u + 1):
                    pass_maxima((r + 1) % QUADS, u + 1)
            quads(sp, quad)

        def attention_pool(pool):
            pool.wait_ge(moe_added, NT)
            pool.memset(k_stk[:], 1.0).then_inc(k_ones, 1)
            pool.memset(v_aug[:], 1.0).then_inc(v_ones, 1)

            def middle(n, w, first):
                pool.wait_ge(rest_got, n * 2 + (w + 1))
                if not first:
                    pool.wait_ge(qk_out[w], n * OUT_RUN)
                pool.sem_inc(passed_pool, 1)
                pool.tensor_copy(parts[:, w, 1, :], rf[:, w, :]).then_inc(mid_got, 1)
            qk_chunks(pool, middle)
            pool.wait_ge(v_got, NG)
            pool.wait_ge(v_ones, 1)

            def values(b, r, u):
                pool.wait_ge(quad_free, u + 1)
                pool.sem_inc(passed_pool, 1)
                pool.tensor_copy(v_aug[:, r, :, :, 0:HD],
                                 v_all[:, bass.ds(b * QT, QT), r * 4 * HD:(r + 1) * 4 * HD].rearrange("p j (h d) -> p j h d", h=4)).then_inc(vaug_in, 1)
            values(0, 0, 0)

            def split_maxima(u):
                pool.wait_ge(max_free, turn_item(u) + 3)
                if not first(u):
                    pool.wait_ge(nm_out, u * DMA)
                pool.sem_inc(passed_pool, 1)
                pool.tensor_copy(nm_parts[:, 0, :], nm[:, 0, :]).then_inc(nm_pool, 1)
                pool.wait_ge(nm_pool, u * 3 + 1)
                pool.tensor_tensor(nm[:, 1, :], nm[:, 0, :], nm_parts[:, 0, :], ALU.subtract).then_inc(nm_pool, 1)
                pool.wait_ge(nm_pool, u * 3 + 2)
                pool.sem_inc(passed_pool, 1)
                pool.tensor_copy(nm_parts[:, 1, :], nm[:, 1, :]).then_inc(nm_pool, 1)
                pool.wait_ge(nm_pool, u * 3 + 3)
                pool.tensor_tensor(nm_parts[:, 2, :], nm[:, 1, :], nm_parts[:, 1, :], ALU.subtract).then_inc(nm_done, 1)

            split_maxima(0)

            def quad(b, r, u):
                if real(u + 1):
                    values(b + (r + 1) // QUADS, (r + 1) % QUADS, u + 1)
                for t in range(NSTEP):
                    if t == NSTEP - MAX_LEAD and real(u + 1):
                        split_maxima(u + 1)
                    if diag(t):
                        for g in range(2):
                            pool.wait_ge(exp_done[g], u * NSTEP + (t + 1))
                            pool.sem_inc(passed_pool, 1)
                            tri = prob[:, t % PRING, g, :, 0:P]
                            pool.affine_select(out=tri, in_=tri, compare_op=ALU.is_ge, fill=0.0, base=0,
                                               pattern=[[0, 2], [1, P]], channel_multiplier=-1).then_inc(causal_done, 1)
            quads(pool, quad)

        def attention_act(act):
            act.wait_ge(small_in, SMALL_LOADS * DMA)

            def high(n, w, first):
                act.wait_ge(qk_put, n * 2 + (w + 1))
                if not first:
                    act.wait_ge(parts_done, n * 2 + (w - 1))
                    act.wait_ge(qk_out[w], n * OUT_RUN)
                act.activation(vf[:, w, :], ps[:, 2 + w, :], ACT.Identity, bias=b_qkv[:, w:w + 1]).then_inc(v32_got, 1)
                act.wait_ge(v32_got, n * 2 + (w + 1))
                act.copy(parts[:, w, 0, :], vf[:, w, :]).then_inc(hi_got, 1)
            qk_chunks(act, high)

            def take_sums(u, c):
                act.wait_ge(prob_free, u * NSTEP + (PRING + (DIAG, NSTEP)[c]))
                act.copy(yraw[:, c, :], ps[:, PV_BANK[c], :]).then_inc(sums_got, 1)

            def step(b, q, u, t):
                n = width(t)
                if real(u):
                    for g in range(2):
                        act.wait_ge(score_mul[g], u * NSTEP + (t + 1))
                        act.wait_ge(prob_free, u * NSTEP + (t + 1))
                        act.activation(prob[:, t % PRING, g, :, 0:n], ps[:, 2 * g:2 * g + 2, 0:n], ACT.Exp,
                                       scale=SCALE).then_inc(exp_done[g], 1)
                if t == 0 and real(u - 1):
                    take_sums(u - 1, 1)
                if t == DIAG and real(u):
                    take_sums(u, 0)
            score_steps(act, step, 2, 2)

            for g in range(NG):
                act.wait_ge(yt_put, g + 1)
                act.copy(zT[:, g * 512:(g + 1) * 512], ps[:, g % 2, :]).then_inc(yt_got, 1)

        def prepare_attention(v, put, own):
            v.wait_ge(wt_put, 1)
            put(v.tensor_copy(w_all[:], ps[:, 6, :]))
            v.tensor_copy(lbT[:], ps[0:R, 7, :]).then_inc(wt_got, 1)
            v.wait_ge(wt_put, 2)
            own()
            v.scalar_tensor_tensor(out=w_all[:], in0=ps[:, 6, :], scalar=LORA_SCALE, in1=w_all[:],
                                   op0=ALU.mult, op1=ALU.add).then_inc(wt_got, 1)

        def attention_dve(v):
            for g in range(NG):
                v.wait_ge(v_mul, g + 1)
                v.tensor_tensor(v_all[:, G4 * g:G4 * (g + 1), :], ps[:, 4 + g % 2, :].rearrange("p (a c) -> p a c", a=G4),
                                bv_all[:].unsqueeze(1).broadcast_to([P, G4, C]), ALU.add).then_inc(v_got, 1)

            def rest(n, w, first):
                v.wait_ge(hi_got, n * 2 + (w + 1))
                v.tensor_tensor(rf[:, w, :], vf[:, w, :], parts[:, w, 0, :], ALU.subtract).then_inc(rest_got, 1)
                v.wait_ge(mid_got, n * 2 + (w + 1))
                v.tensor_tensor(parts[:, w, 2, :], rf[:, w, :], parts[:, w, 1, :], ALU.subtract).then_inc(parts_done, 1)
            qk_chunks(v, rest)

            def maxima(u, r, chunks):
                for n in chunks:
                    i, kc, pr, hh = CHUNKS[n]
                    keys = min(512, (i + 1) * P - kc * 512)
                    item = chunk_item(u, n)
                    v.wait_ge(max_mul, item + 1)
                    bank = ps[:, chunk_bank(u, r, n), 0:keys]
                    h = 2 * pr + hh
                    if kc == i // DIAG:
                        v.wait_ge(max_free, item + 1)
                        v.sem_inc(passed, 1)
                        v.tensor_tensor_reduce(out=junk[:, n % 2, 0:keys], in0=bank, in1=causal[:, 512 - keys:512], scale=1.0,
                                               scalar=LOWEST, op0=ALU.add, op1=ALU.max,
                                               accum_out=mx[:, r % 2, h, i:i + 1]).then_inc(max_free, 1)
                    else:
                        v.tensor_reduce(mx0[:, h, i:i + 1], bank, AX_X, ALU.max).then_inc(max_free, 1)

            def join_maxima(u, r):
                v.wait_ge(max_free, chunk_item(u, NP1 - 1) + 3)
                both = mx[:, r % 2, :, DIAG:]
                v.tensor_tensor(both, both, mx0[:, :, DIAG:], ALU.max).then_inc(max_done, 1)

            def negate_maxima(u, r):
                if not first(u):
                    v.wait_ge(nm_done, u)
                v.wait_ge(max_mul, turn_item(u) + 1)
                v.tensor_scalar(nm[:, 0, :], ps[0:4 * QT, turn_bank(u, r), 0:P], -1.0, None, ALU.mult).then_inc(max_free, 1)

            def divide(b, q, u, c):
                r = q % QUADS
                v.wait_ge(turned, u * NCH + (c + 1))
                sums = ps[:, PV_BANK[c], :].rearrange("p (a h d) -> p a h d", a=DIAG, h=4)
                v.reciprocal(rden[:, c], sums[:, :, :, HD]).then_inc(rden_done, 1)
                v.wait_ge(rden_done, u * NCH + (c + 1))
                t0 = (b + (q - r) // QUADS) * QT + DIAG * c
                v.tensor_tensor(z_sb[:, bass.ds(t0, DIAG), r * 4 * HD:(r + 1) * 4 * HD].rearrange("p a (h d) -> p a h d", h=4),
                                sums[:, :, :, 0:HD], rden[:, c].unsqueeze(3).broadcast_to([P, DIAG, 4, HD]), ALU.mult).then_inc(pv_free[c], 1)

            maxima(0, 0, range(NP1))
            join_maxima(0, 0)
            maxima(1, 1, range(MAX_PER))
            negate_maxima(0, 0)
            maxima(1, 1, range(MAX_PER, MAX_PER * MAX_LEAD))

            def step(b, q, u, t):
                ahead, chunks = max_chunks(t)
                if real(u + ahead):
                    maxima(u + ahead, (q + ahead) % QUADS, chunks)
                if t == NSTEP - MAX_LEAD - 1 and real(u + 1):
                    join_maxima(u + 1, (q + 1) % QUADS)
                if t == NSTEP - MAX_LEAD and real(u + 1):
                    negate_maxima(u + 1, (q + 1) % QUADS)
                if t == 2 and real(u - 1):
                    divide(b, q - 1, u - 1, 1)
                if t == DIAG + 2 and real(u):
                    divide(b, q, u, 0)
            score_steps(v, step, 4, 4)

            for g in range(NG):
                v.wait_ge(proj_mul, g + 1)
                xg = x_sb[:, G4 * g:G4 * (g + 1), :]
                v.tensor_tensor(xg, ps[:, 2 + g % 2, :].rearrange("p (a c) -> p a c", a=G4), xg, ALU.add).then_inc(proj_sum, 1)
                v.wait_ge(proj_sum, g + 1)
                v.tensor_tensor(xg, xg, bp_all[:].unsqueeze(1).broadcast_to([P, G4, C]), ALU.add).then_inc(att_added, 1)
            v.wait_ge(att_added, NG)

        def attention_pe_weights(pe):
            pe.wait_ge(small_in, SMALL_LOADS * DMA)
            pe.wait_ge(y_got, NS)
            for j in range(3):
                pe.transpose(ps[:, 6, j * P:(j + 1) * P], wattn_in[:, j, :], ident[:])
                pe.transpose(ps[0:R, 7, j * P:(j + 1) * P], lb_in[:, j, :], ident[:])
            pe.transpose(ps[:, 6, 3 * P:4 * P], wproj_in[:], ident[:])
            pe.transpose(ps[0:R, 7, 3 * P:4 * P], lbp_in[:], ident[:]).then_inc(wt_put, 1)
            pe.wait_ge(wt_got, 1)
            pe.matmul(ps[:, 6, 0:3 * C], la_in[:], lbT[:, 0:3 * C], start=True, stop=True)
            pe.matmul(ps[:, 6, 3 * C:], lap_in[:], lbT[:, 3 * C:], start=True, stop=True).then_inc(wt_put, 1)

        def attention_pe(pe):
            pe.wait_ge(wt_got, 2)
            pe.sem_inc(quad_free, 4)
            pe.sem_inc(max_free, 2)
            for c in range(NCH):
                pe.sem_inc(pv_free[c], 1)
            pe.sem_inc(prob_free, PRING)
            pe.wait_ge(zt_got, 2 * NG)
            for g in range(NG):
                if g >= 2:
                    pe.wait_ge(v_got, g - 1)
                for a in range(G4):
                    t = G4 * g + a
                    mm = pe.matmul(ps[:, 4 + g % 2, a * C:(a + 1) * C], zT[:, t * P:(t + 1) * P], w_all[:, 2 * C:3 * C], start=True, stop=True)
                mm.then_inc(v_mul, 1)

            def project(n, w, first):
                if not first:
                    pe.wait_ge(v32_got, n * 2 + (w - 1))
                pe.matmul(ps[:, 2 + w, :], w_all[:, w * C:(w + 1) * C], zT[:, bass.ds(n * CW, CW)], start=True, stop=True).then_inc(qk_put, 1)
            qk_chunks(pe, project)
            pe.wait_ge(v32_got, 2 * NQK)
            pe.wait_ge(v_got, NG)

            def max_scores(u, r, chunks):
                for n in chunks:
                    i, kc, pr, hh = CHUNKS[n]
                    keys = min(512, (i + 1) * P - kc * 512)
                    rows = slice(64 * hh, 64 * hh + SR)
                    pe.wait_ge(max_free, chunk_item(u, n) + 1)
                    pe.matmul(ps[:, chunk_bank(u, r, n), 0:keys], q_stk[rows, r, pr, i * P:(i + 1) * P],
                              k_stk[rows, r, pr, kc * 512:kc * 512 + keys], start=True, stop=True).then_inc(max_mul, 1)

            def turn_maxima(u, r):
                pe.wait_ge(max_done, u + 1)
                pe.wait_ge(max_free, turn_item(u) + 1)
                pe.transpose(ps[0:4 * QT, turn_bank(u, r), 0:P], mx[:, r % 2, :, :].rearrange("p h i -> p (h i)"),
                             ident[:]).then_inc(max_mul, 1)

            def scores(u, r, t, g):
                c, j = STEPS[t]
                n = width(t)
                if t == 0 and g == 0:
                    pe.wait_ge(nm_in, (u + 1) * 2 * DMA)
                if not (isinstance(u, int) and u == 0 and t == 0):
                    pe.wait_ge(exp_done[g], u * NSTEP + t)
                for hh in range(2):
                    rows = slice(64 * hh, 64 * hh + KR)
                    mm = pe.matmul(ps[:, 2 * g + hh, 0:n], k_stk[rows, r, g, j * P:(j + 1) * P],
                                   q_stk[rows, r, g, (c + 1) * CW - n:(c + 1) * CW], start=True, stop=True)
                mm.then_inc(score_mul[g], 1)

            def weigh(u, r, t):
                c, j = STEPS[t]
                n = width(t)
                for g in range(2):
                    pe.wait_ge(exp_done[g], u * NSTEP + (t + 1))
                if diag(t):
                    d = sum(diag(s) for s in range(t + 1))
                    pe.wait_ge(causal_done, u * 2 * NDIAG + 2 * d)
                if t == 0:
                    pe.wait_ge(vaug_in, u + 1)
                if j == 0:
                    pe.wait_ge(pv_free[c], u + 1)
                for h in range(4):
                    mm = pe.matmul(ps[32 * h:32 * h + 32, PV_BANK[c], CW - n:CW], v_aug[:, r, j, h, :],
                                   prob[:, t % PRING, h // 2, h % 2, 0:n], start=(j == 0), stop=(j == DIAG * (c + 1) - 1))
                mm.then_inc(prob_free, 1)

            def turn_out(u, c):
                pe.wait_ge(sums_got, u * NCH + (c + 1))
                for a in range(DIAG):
                    mm = pe.transpose(ps[:, PV_BANK[c], a * P:(a + 1) * P], yraw[:, c, a * P:(a + 1) * P], ident[:])
                    if c == NCH - 1 and a == 0:
                        mm.then_inc(quad_free, 1)
                mm.then_inc(turned, 1)

            pe.wait_ge(stack_in[0], 4 * DMA)
            max_scores(0, 0, range(NP1))
            pe.wait_ge(stack_in[1], 4 * DMA)
            max_scores(1, 1, range(MAX_PER))
            turn_maxima(0, 0)
            max_scores(1, 1, range(MAX_PER, MAX_PER * MAX_LEAD))
            for g in range(2):
                scores(0, 0, 0, g)

            def step(b, q, u, t):
                nq, nt = divmod(q * NSTEP + t + 1, NSTEP)
                nu = u + (nq - q)
                if t == NSTEP - MAX_LEAD and real(u + 2):
                    pe.wait_ge(stack_in[(q + 2) % QUADS], (b + ((q + 2) // QUADS + 1)) * 4 * DMA)

                def some_max(at, part):
                    ahead, chunks = max_chunks(at)
                    if real(u + ahead):
                        max_scores(u + ahead, (q + ahead) % QUADS, chunks[part])

                odd = t % 2
                for g in range(2):
                    if real(nu):
                        scores(nu, nq % QUADS, nt, g)
                    some_max(t - odd, slice(g + 2 * odd, g + 2 * odd + 1))
                if odd:
                    if real(u):
                        weigh(u, q % QUADS, t - 1)
                    if t - 1 == NSTEP - MAX_LEAD and real(u + 1):
                        turn_maxima(u + 1, (q + 1) % QUADS)
                    some_max(t, slice(0, 2))
                    if real(u):
                        weigh(u, q % QUADS, t)
                    some_max(t, slice(2, 4))
                if t == 1 and real(u - 1):
                    turn_out(u - 1, 1)
                if t == DIAG + 1 and real(u):
                    turn_out(u, 0)
            score_steps(pe, step, 2, 2)

            def proj(g):
                pe.wait_ge(yt_got, g + 1)
                if g >= 2:
                    pe.wait_ge(proj_sum, g - 1)
                for a in range(G4):
                    t = G4 * g + a
                    mm = pe.matmul(ps[:, 2 + g % 2, a * C:(a + 1) * C], zT[:, t * P:(t + 1) * P], w_all[:, 3 * C:], start=True, stop=True)
                mm.then_inc(proj_mul, 1)
            for c in range(NCH):
                pe.wait_ge(pv_free[c], NQ + 1)
            for g in range(NG):
                if g >= 2:
                    pe.wait_ge(yt_got, g - 1)
                for a in range(G4):
                    mm = pe.transpose(ps[:, g % 2, a * P:(a + 1) * P], z_sb[:, G4 * g + a, :], ident[:])
                mm.then_inc(yt_put, 1)
                if g >= 1:
                    proj(g - 1)
            proj(NG - 1)

        def transposes(pe, n):
            for g in range(NG):
                pe.wait_ge(z_ready, NG * n + g + 1)
                if g >= 2:
                    pe.wait_ge(zt_got, NG * n + g - 1)
                for a in range(G4):
                    mm = pe.transpose(ps[:, g % 2, a * P:(a + 1) * P], z_sb[:, G4 * g + a, :], ident[:])
                mm.then_inc(zt_put, 1)
                yield g

        def take_transposes(act, n):
            for g in range(NG):
                act.wait_ge(zt_put, NG * n + g + 1)
                act.copy(zT[:, g * 512:(g + 1) * 512], ps[:, g % 2, :]).then_inc(zt_got, 1)

        @block.sync
        def _(sp):
            sp.dma_start(x_sb[:, 0:8, :], x_dram[:, 0:8, :]).then_inc(x_in[0], DMA)
            sp.dma_start(wg_in[:], wg).then_inc(gate_in, DMA)
            sp.dma_start(wgred_in[:], wg_red).then_inc(gate_in, DMA)
            for g in range(1, 4):
                sp.dma_start(x_sb[:, 8 * g:8 * g + 8, :], x_dram[:, 8 * g:8 * g + 8, :]).then_inc(x_in[g], DMA)
            sp.dma_start(bias_in[:, 0:BW1], b1.rearrange("e f -> (e f)").rearrange("(p n) -> p n", p=P)).then_inc(bias_i, DMA)
            sp.dma_start(bias_in[:, BW1:BF_W], b2.rearrange("e f -> (e f)").rearrange("(p n) -> p n", p=P)).then_inc(bias_i, DMA)
            sp.wait_ge(zeros_done, 1)
            sp.dma_start(slots.rearrange("(j p) c -> p j c", p=P), gath[:, 0:1, :].broadcast_to([P, NS, C])).then_inc(slots_clear, DMA)
            sp.dma_start(w1_sb[:], w1.rearrange("e c f -> c e f")).then_inc(w1_in, DMA)
            sp.dma_start(w2_sb[:], w2.rearrange("e (k p) c -> p e k c", p=P)).then_inc(w2_in, DMA)
            sp.wait_ge(bias_split, 1)
            for k in range(3):
                sp.dma_start(bias_d[k, 0:E * F].rearrange("(p n) -> p n", p=P), bias_parts[:, k, 0:BW1]).then_inc(bias_out, DMA)
                sp.dma_start(bias_d[k, E * F:].rearrange("(p n) -> p n", p=P), bias_parts[:, k, BW1:BF_W]).then_inc(bias_out, DMA)
            sp.wait_ge(bias_out, 6 * DMA)
            sp.wait_ge(consts, CONSTS)
            sp.dma_start(b1_rows[0:3, :], bias_d[:, 0:E * F]).then_inc(bias_back, DMA)
            sp.dma_start(b2_rows[0:3, :], bias_d[:, E * F:]).then_inc(bias_back, DMA)
            sp.dma_start(wattn_in[:], w_attn.rearrange("(j p) c -> p j c", p=P)).then_inc(small_in, DMA)
            sp.dma_start(la_in[:], la_attn).then_inc(small_in, DMA)
            sp.dma_start(lb_in[:], lb_attn.rearrange("(j p) r -> p j r", p=P)).then_inc(small_in, DMA)
            sp.dma_start(wproj_in[:], w_proj).then_inc(small_in, DMA)
            sp.dma_start(lap_in[:], la_proj).then_inc(small_in, DMA)
            sp.dma_start(lbp_in[:], lb_proj).then_inc(small_in, DMA)
            with nc.allow_non_contiguous_dma(reason="three bias values per partition"):
                sp.dma_start(b_qkv[:], b_attn.rearrange("(j p) -> p j", p=P)).then_inc(small_in, DMA)
            sp.dma_start(bv_all[:], b_attn[2 * C:].rearrange("(o c) -> o c", o=1).broadcast_to([P, C])).then_inc(small_in, DMA)
            sp.dma_start(bp_all[:], b_proj.rearrange("(o c) -> o c", o=1).broadcast_to([P, C])).then_inc(small_in, DMA)

            def moe(f):
                def step(s, r, turn):
                    if not runs(s, 0):
                        return
                    if later(s, 4):
                        sp.wait_ge(xt_put, s + (f * NS - 3))
                    sp.dma_start(xin[:, r, :], slots[bass.ds(s * P, P), :]).then_inc(slot_in[r], DMA)
                sp.wait_ge(scattered, (f + 1) * NT * DMA)
                tile_steps(sp, step)

            moe(0)
            attention_sp(sp)
            moe(1)
            for g in range(4):
                sp.wait_ge(moe_added, NT + 8 * (g + 1))
                sp.dma_start(out_dram[:, 8 * g:8 * g + 8, :], x_sb[:, 8 * g:8 * g + 8, :]).then_inc(out_done, DMA)
            sp.wait_ge(out_done, 4 * DMA)

        @block.gpsimd
        def _(pool):
            pool.memset(gath[:, 0, :], 0.0).then_inc(zeros_done, 1)
            pool.memset(ident[:], 0.0).then_inc(consts, 1)
            pool.memset(ones_bf[:], 1.0).then_inc(consts, 1)
            pool.memset(before[:], 1.0).then_inc(consts, 1)
            pool.memset(causal[:], 0.0).then_inc(consts, 1)
            pool.memset(scanA[:], 0.0).then_inc(consts, 1)
            pool.memset(scanB[:], 0.0).then_inc(consts, 1)
            pool.memset(padA[:], 0.0).then_inc(consts, 1)
            pool.memset(padB[:], 0.0).then_inc(consts, 1)
            pool.memset(b1_rows[:].bitcast(F32), 0.0).then_inc(consts, 1)
            pool.memset(b2_rows[:].bitcast(F32), 0.0).then_inc(consts, 1)
            pool.memset(minus_half[:], -0.5).then_inc(consts, 1)
            pool.iota(rev[:], [[-1, E]], base=E, channel_multiplier=0, allow_small_or_imprecise_dtypes=True).then_inc(consts, 1)
            pool.iota(starts[:], [[P, NS]], base=0, channel_multiplier=0, allow_small_or_imprecise_dtypes=True).then_inc(consts, 1)
            pool.wait_ge(consts, CONSTS - 3)
            pool.affine_select(out=ident[:], in_=ident[:], compare_op=ALU.not_equal, fill=1.0, base=0,
                               pattern=[[-1, P]], channel_multiplier=1).then_inc(consts, 1)
            pool.affine_select(out=before[:], in_=before[:], compare_op=ALU.is_gt, fill=0.0, base=0,
                               pattern=[[1, P]], channel_multiplier=-1).then_inc(consts, 1)
            pool.affine_select(out=causal[:, 384:512], in_=causal[:, 384:512], compare_op=ALU.is_ge, fill=LOWEST, base=0,
                               pattern=[[-1, P]], channel_multiplier=1).then_inc(consts, 1)

            def moe(f):
                pool.wait_ge(pos_done, f + 1)
                if f == 0:
                    pool.wait_ge(slots_clear, DMA)
                for a in range(NT):
                    pool.indirect_dma_start(
                        out=slots, out_offset=bass.IndirectOffsetOnAxis(ap=pos[:, a:a + 1].bitcast(U32), axis=0),
                        in_=z_sb[:, a, :], in_offset=None, bounds_check=NS * P - 1).then_inc(scattered, DMA)
                for r in range(4):
                    pool.wait_ge(y_out[r], (f + 1) * per_ring(r) * DMA)
                for a in range(NT):
                    pool.indirect_dma_start(
                        out=gath[:, a, :], out_offset=None, in_=yslots,
                        in_offset=bass.IndirectOffsetOnAxis(ap=pos[:, a:a + 1].bitcast(U32), axis=0),
                        bounds_check=NS * P - 1).then_inc(gathered[a // 8], DMA)

            def deviation(n):
                pool.wait_ge(root_in, n + 2)
                pool.tensor_tensor(rstd[:], lnw[:, 5, :], minus_half[:], ALU.pow).then_inc(root_done, 1)

            pool.wait_ge(root_in, 1)
            pool.tensor_tensor(wg_n[:, 1:2], wg_n[:, 0:1], minus_half[0:E, 0:1], ALU.pow).then_inc(root_done, 1)
            deviation(0)
            moe(0)
            deviation(1)
            attention_pool(pool)
            deviation(2)
            moe(1)

        @block.vector
        def _(v):
            n_dve = [0]

            def put(ins):
                n_dve[0] += 1
                ins.then_inc(dve, 1)

            def own():
                v.wait_ge(dve, n_dve[0])

            def square_gate():
                v.wait_ge(gate_in, 2 * DMA)
                v.tensor_tensor_reduce(out=wg_sq[:], in0=wg_in[:], in1=wg_in[:], scale=1.0, scalar=0.0,
                                       op0=ALU.mult, op1=ALU.add, accum_out=wg_n[:, 0:1]).then_inc(root_in, 1)

            def prepare():
                v.wait_ge(root_done, 1)
                put(v.tensor_scalar(wg_n[:, 2:3], wg_n[:, 1:2], 1.0 / NORM_EPS, None, ALU.min))
                own()
                v.tensor_scalar(wg_unit[:], wg_in[:], wg_n[:, 2:3], None, ALU.mult).then_inc(gate_sub, 1)
                v.wait_ge(bias_i, 2 * DMA)
                put(v.tensor_copy(bias_parts[:, 0, :], bias_in[:]))
                own()
                put(v.tensor_tensor(bias_r[:, 0, :], bias_in[:], bias_parts[:, 0, :], ALU.subtract))
                own()
                put(v.tensor_copy(bias_parts[:, 1, :], bias_r[:, 0, :]))
                own()
                v.tensor_tensor(bias_parts[:, 2, :], bias_r[:, 0, :], bias_parts[:, 1, :], ALU.subtract).then_inc(bias_split, 1)
                v.wait_ge(wprep_pe, 1)
                v.tensor_copy(wgT[:], ps[0:GD, 2, 0:E]).then_inc(wprep_got, 1)
                v.wait_ge(wprep_pe, 2)
                v.tensor_copy(wgate[:], ps[:, 2, 0:E]).then_inc(wprep_got, 1)

            def layer_norm(n):
                with v.Fori(0, NG) as g:
                    for a in range(G4):
                        last = v.bn_stats(stats[:, bass.ds(g * G4 + a, 1), :].rearrange("p a c -> p (a c)"),
                                          x_sb[:, bass.ds(g * G4 + a, 1), :].rearrange("p a c -> p (a c)"))
                    last.then_inc(bn_done, 1)
                v.wait_ge(bn_done, NG * (n + 1))
                me, mo, qe, qo = (stats[:, :, k] for k in (1, 4, 2, 5))
                put(v.tensor_tensor(lnw[:, 0, :], me, mo, ALU.add))
                put(v.tensor_tensor(lnw[:, 1, :], me, mo, ALU.subtract))
                put(v.tensor_tensor(lnw[:, 2, :], qe, qo, ALU.add))
                own()
                put(v.tensor_scalar(mean[:], lnw[:, 0, :], 0.5, None, ALU.mult))
                put(v.tensor_tensor(lnw[:, 3, :], lnw[:, 1, :], lnw[:, 1, :], ALU.mult))
                put(v.tensor_scalar(lnw[:, 4, :], lnw[:, 2, :], 1.0 / C, LN_EPS, ALU.mult, ALU.add))
                own()
                v.scalar_tensor_tensor(out=lnw[:, 5, :], in0=lnw[:, 3, :], scalar=0.25, in1=lnw[:, 4, :],
                                       op0=ALU.mult, op1=ALU.add).then_inc(root_in, 1)
                v.wait_ge(root_done, n + 2)
                with v.Fori(0, NG) as g:
                    for a in range(G4):
                        t = g * G4 + a
                        last = v.tensor_scalar(z_sb[:, bass.ds(t, 1), :].rearrange("p a c -> p (a c)"),
                                               x_sb[:, bass.ds(t, 1), :].rearrange("p a c -> p (a c)"),
                                               mean[:, bass.ds(t, 1)], rstd[:, bass.ds(t, 1)], ALU.subtract, ALU.mult)
                    last.then_inc(z_ready, 1)

            def over_e(t):
                return t.unsqueeze(2).broadcast_to([P, NT, E])

            def route(f):
                v.wait_ge(logits_done, f + 1)
                put(v.tensor_copy(logit[:], ps[:, 7, 0:NT * E].rearrange("p (a e) -> p a e", e=E)))
                own()
                put(v.tensor_reduce(gmax[:, 0, :], logit[:], AX_X, ALU.max))
                own()
                v.tensor_tensor(gtmp[:], logit[:], over_e(gmax[:, 0, :]), ALU.subtract).then_inc(gate_sub, 1)
                put(v.tensor_tensor(logit[:], logit[:], over_e(gmax[:, 0, :]), ALU.is_equal))
                own()
                put(v.tensor_tensor(logit[:], logit[:], rev[:].unsqueeze(1).broadcast_to([P, NT, E]), ALU.mult))
                own()
                put(v.tensor_reduce(gmax[:, 1, :], logit[:], AX_X, ALU.max))
                own()
                v.tensor_tensor(onehot[:], logit[:], over_e(gmax[:, 1, :]), ALU.is_equal).then_inc(onehot_done, 1)
                v.wait_ge(gate_exp, f + 1)
                put(v.tensor_reduce(gmax[:, 2, :], gexp[:], AX_X, ALU.add))
                own()
                put(v.reciprocal(score[:], gmax[:, 2, :]))
                own()
                put(v.tensor_scalar(score[:], score[:], BRANCH, None, ALU.mult))
                v.wait_ge(counted, f + 1)
                H = NT // 2
                tot = ps[:, 6, NT * E:2 * NT * E].rearrange("p (a e) -> p a e", e=E)
                front = ps[:, 6, 0:NT * E].rearrange("p (a e) -> p a e", e=E)
                put(v.tensor_copy(scanA[:, H:, :], tot))
                own()
                src, dst, d = scanA, scanB, 1
                while d < NT:
                    put(v.tensor_tensor(dst[:, H:, :], src[:, H:, :], src[:, H - d:H + NT - d, :], ALU.add))
                    own()
                    src, dst, d = dst, src, 2 * d
                put(v.tensor_scalar(cnt_i[:, 0, :], src[:, H + NT - 1, :], float(P - 1), None, ALU.add))
                own()
                SH = P.bit_length() - 1
                put(v.tensor_scalar(cnt_i[:, 1, :], cnt_i[:, 0, :], SH, SH, ALU.logical_shift_right, ALU.logical_shift_left))
                own()
                put(v.tensor_copy(padA[:, E // 2:], cnt_i[:, 1, :]))
                own()
                put(v.tensor_scalar(ebase[:], padA[:, E // 2:], -1.0, None, ALU.mult))
                a, b, d = padA, padB, 1
                while d < E:
                    put(v.tensor_tensor(b[:, E // 2:], a[:, E // 2:], a[:, E // 2 - d:E // 2 + E - d], ALU.add))
                    own()
                    a, b, d = b, a, 2 * d
                ends = a[:, E // 2:]
                put(v.tensor_tensor(ebase[:], ebase[:], ends, ALU.add))
                put(v.tensor_tensor(slot_of[:], src[:, H:, :], tot, ALU.subtract))
                own()
                put(v.tensor_tensor(slot_of[:], slot_of[:], front, ALU.add))
                own()
                put(v.tensor_tensor(slot_of[:], slot_of[:], ebase[:].unsqueeze(1).broadcast_to([P, NT, E]), ALU.add))
                own()
                put(v.tensor_tensor(slot_of[:], slot_of[:], onehot[:], ALU.mult))
                own()
                put(v.tensor_reduce(pos_f[:], slot_of[:], AX_X, ALU.add))
                own()
                v.tensor_copy(pos[:], pos_f[:]).then_inc(pos_done, 1)
                put(v.tensor_tensor(ecmp[:], starts[:].unsqueeze(2).broadcast_to([1, NS, E - 1]),
                                    ends[0:1, 0:E - 1].unsqueeze(1).broadcast_to([1, NS, E - 1]), ALU.is_ge))
                own()
                put(v.tensor_reduce(etab_f[:], ecmp[:], AX_X, ALU.add))
                own()
                v.tensor_copy(etab[:], etab_f[:]).then_inc(etab_done, 1)

            def experts(f):
                base = f * NS

                def step(s, r, turn):
                    if runs(s, 0):
                        v.wait_ge(xt_put, s + (base + 1))
                        if later(s, 2):
                            v.wait_ge(up_done, s + (base - 1))
                        v.tensor_copy(xs[:, r % 2, :], ps[:, r % 2, 0:P]).then_inc(xt_got, 1)
                    if runs(s, 2):
                        v.wait_ge(ht_put, s + (base - 1))
                        if later(s, 4):
                            v.wait_ge(down_done, s + (base - 3))
                        v.tensor_copy(hT[:, r % 2, :, :], ps[:, 4 + r % 2, :].rearrange("p (k c) -> p k c", k=FK)).then_inc(ht_got, 1)

                tile_steps(v, step)
                for g in range(4):
                    v.wait_ge(gathered[g], (f + 1) * 8 * DMA)
                    for a in range(8 * g, 8 * g + 8):
                        v.scalar_tensor_tensor(out=x_sb[:, a, :], in0=gath[:, a, :], scalar=score[:, a:a + 1],
                                               in1=x_sb[:, a, :], op0=ALU.mult, op1=ALU.add).then_inc(moe_added, 1)

            v.wait_ge(consts, CONSTS)
            square_gate()
            for g in range(4):
                v.wait_ge(x_in[g], DMA)
            layer_norm(0)
            prepare()
            route(0)
            experts(0)
            v.wait_ge(moe_added, NT)
            prepare_attention(v, put, own)
            layer_norm(1)
            attention_dve(v)
            layer_norm(2)
            route(1)
            experts(1)

        @block.scalar
        def _(act):
            def gate(f):
                act.wait_ge(gate_sub, f + 2)
                act.activation(gexp[:], gtmp[:], ACT.Exp).then_inc(gate_exp, 1)

            def experts(f):
                base = f * NS

                def step(s, r, turn):
                    if runs(s, 1):
                        act.wait_ge(up_done, s + base)
                        if later(s, 3):
                            act.wait_ge(ht_put, s + (base - 2))
                        act.activation(hid[:, (r - 1) % 2, :], ps[:, 2 + (r - 1) % 2, :], ACT.Gelu).then_inc(gelu_done, 1)
                    if runs(s, 3):
                        act.wait_ge(down_done, s + (base - 2))
                        q = (r - 3) % 4
                        full = turn if r == 3 else turn - 1
                        if not isinstance(full, int) or full > 0:
                            act.wait_ge(y_out[q], (full + f * per_ring(q)) * DMA)
                        act.copy(yr[:, q, :], ps[:, 6 + (r - 3) % 2, 0:C]).then_inc(y_got, 1)
                        act.wait_ge(y_got, s + (base - 2))
                        act.dma_start(yslots[bass.ds((s - 3) * P, P), :], yr[:, q, :]).then_inc(y_out[q], DMA)

                tile_steps(act, step)

            take_transposes(act, 0)
            gate(0)
            experts(0)
            take_transposes(act, 1)
            attention_act(act)
            take_transposes(act, 2)
            gate(1)
            experts(1)

        @block.tensor
        def _(pe):
            def prepare():
                pe.wait_ge(consts, CONSTS)
                pe.wait_ge(gate_sub, 1)
                pe.transpose(ps[0:GD, 2, 0:E], wg_unit[:], ident[0:E, 0:E]).then_inc(wprep_pe, 1)
                pe.wait_ge(wprep_got, 1)
                pe.matmul(ps[:, 2, 0:E], wgred_in[:], wgT[:], start=True, stop=True).then_inc(wprep_pe, 1)
                pe.wait_ge(wprep_got, 2)

            def gate(f, n):
                def logits(g):
                    pe.wait_ge(zt_got, NG * n + g + 1)
                    for a in range(G4 * g, G4 * g + G4):
                        mm = pe.matmul(ps[:, 7, a * E:(a + 1) * E], zT[:, a * P:(a + 1) * P], wgate[:], start=True, stop=True)
                    return mm
                for g in transposes(pe, n):
                    if g >= 1:
                        logits(g - 1)
                logits(NG - 1).then_inc(logits_done, 1)
                pe.wait_ge(onehot_done, f + 1)
                oh = onehot[:].rearrange("p a e -> p (a e)")
                pe.matmul(ps[:, 6, 0:NT * E], before[:], oh, start=True, stop=True)
                pe.matmul(ps[:, 6, NT * E:2 * NT * E], ones_bf[:], oh, start=True, stop=True).then_inc(counted, 1)

            def experts(f):
                base = f * NS
                pe.wait_ge(etab_done, f + 1)
                if f == 0:
                    pe.wait_ge(w1_in, DMA)
                    pe.wait_ge(w2_in, DMA)
                    pe.wait_ge(bias_back, 2 * DMA)

                def step(s, r, turn):
                    if runs(s, 0):
                        pe.wait_ge(slot_in[r], (turn + (f * per_ring(r) + 1)) * DMA)
                        if later(s, 2):
                            pe.wait_ge(xt_got, s + (base - 1))
                        pe.transpose(ps[:, r % 2, 0:P], xin[:, r, :], ident[:]).then_inc(xt_put, 1)
                    if runs(s, 1):
                        b = 2 + (r - 1) % 2
                        e = pe.value_load(etab[0:1, bass.ds(s - 1, 1)], min_val=0, max_val=E - 1)
                        pe.wait_ge(xt_got, s + base)
                        if later(s, 3):
                            pe.wait_ge(gelu_done, s + (base - 2))
                        pe.matmul(ps[:, b, :], xs[:, (r - 1) % 2, :], w1_sb[:, bass.ds(e, 1), :].rearrange("p e f -> p (e f)"),
                                  start=True, stop=False)
                        pe.matmul(ps[:, b, :], ones_bf[:], b1_rows[:, bass.ds(e * F, F)], start=False, stop=True).then_inc(up_done, 1)
                    if runs(s, 2):
                        b = 4 + r % 2
                        pe.wait_ge(gelu_done, s + (base - 1))
                        if later(s, 4):
                            pe.wait_ge(ht_got, s + (base - 3))
                        for k in range(FK):
                            mm = pe.transpose(ps[:, b, k * P:(k + 1) * P], hid[:, r % 2, k * P:(k + 1) * P], ident[:])
                        mm.then_inc(ht_put, 1)
                    if runs(s, 3):
                        b = 6 + (r - 3) % 2
                        e = pe.value_load(etab[0:1, bass.ds(s - 3, 1)], min_val=0, max_val=E - 1)
                        pe.wait_ge(ht_got, s + (base - 2))
                        if later(s, 5):
                            pe.wait_ge(y_got, s + (base - 4))
                        for k in range(FK):
                            pe.matmul(ps[:, b, 0:C], hT[:, (r - 3) % 2, k, :], w2_sb[:, bass.ds(e, 1), k, :].rearrange("p e c -> p (e c)"),
                                      start=(k == 0), stop=False)
                        pe.matmul(ps[:, b, 0:C], ones_bf[:], b2_rows[:, bass.ds(e * C, C)], start=False, stop=True).then_inc(down_done, 1)

                tile_steps(pe, step)

            prepare()
            gate(0, 0)
            experts(0)
            attention_pe_weights(pe)
            for _ in transposes(pe, 1):
                pass
            attention_pe(pe)
            gate(1, 2)
            experts(1)


_INS = ['L0_attn_x', 'L0_attn_w_attn', 'L0_attn_b_attn', 'L0_attn_la_attn', 'L0_attn_lb_attn', 'L0_attn_w_proj',
        'L0_attn_b_proj', 'L0_attn_la_proj', 'L0_attn_lb_proj', 'L0_ffn_wg_red', 'L0_ffn_wg', 'L0_ffn_w1',
        'L0_ffn_b1', 'L0_ffn_w2', 'L0_ffn_b2']


def kernel(**inputs):
    import numpy as _np
    import concourse.bacc as _bacc
    from concourse import mybir as _mybir
    from concourse.bass_utils import run_bass_kernel_spmd as _run

    nc = _bacc.Bacc("TRN2", target_bir_lowering=False, num_devices=1)
    arrays, args = {}, []
    for name in _INS:
        a = _np.ascontiguousarray(inputs[name])
        arrays[f"in_{name}_dram"] = a
        args.append(nc.dram_tensor(f"in_{name}_dram", a.shape, _mybir.dt.from_np(a.dtype), kind="ExternalInput").ap())
    shape = inputs["L0_attn_x"].shape
    args.append(nc.dram_tensor("out_0_dram", shape, _mybir.dt.float32, kind="ExternalOutput").ap())
    macaron_kernel(nc, *args)
    r = _run(nc, [arrays], core_ids=[0])
    return r.results[0]["out_0_dram"]
```

```python
from contextlib import ExitStack

import concourse.bass as bass
from concourse import mybir

P = 128
ALU = mybir.AluOpType
ACT = mybir.ActivationFunctionType
F32 = mybir.dt.float32
BF16 = mybir.dt.bfloat16
I32 = mybir.dt.int32
U32 = mybir.dt.uint32
AX_X = mybir.AxisListType.X

LN_EPS = 1e-5
NORM_EPS = 1e-4
LORA_SCALE = 0.5
BRANCH = 0.5
LOWEST = -3.0e38
HEADS = 16
G4 = 4
DMA = 16

Q_PARTS = (0, 0, 0, 1, 1, 1, 2)
K_PARTS = (0, 1, 2, 0, 1, 2, 0)
STACK_RUNS = 3


def macaron_kernel(nc, x, w_attn, b_attn, la_attn, lb_attn, w_proj, b_proj, la_proj, lb_proj,
                   wg_red, wg, w1, b1, w2, b2, out):
    B, T, C = x.shape
    N = B * T
    NT = N // P
    NG = NT // G4
    E, _, F = w1.shape
    FK = F // P
    GD = wg.shape[1]
    R = la_attn.shape[0]
    NS = NT + E - 1
    HD = C // HEADS
    SCALE = float(HD) ** -0.5
    QUADS = HEADS // 4
    QT = T // P
    CW = 512
    NCH = T // CW
    DIAG = CW // P
    SR = len(Q_PARTS) * HD
    KR = SR + 3
    STEPS = [(c, j) for c in range(NCH) for j in range(DIAG * (c + 1))]
    NSTEP = len(STEPS)
    CHUNKS = []
    for i in range(QT):
        for kc in range(i // DIAG + 1):
            keys = min(512, (i + 1) * P - kc * 512)
            heads = ((0, 2), (1, 3)) if 2 * keys <= 512 else ((0,), (1,), (2,), (3,))
            CHUNKS += [(i, kc, h, keys) for h in heads]
    NP1 = len(CHUNKS)
    TURN_AT = 2
    MAX_START = NSTEP // 2
    MAX_ITEMS = NP1 + 1
    NQ = B * QUADS
    PRING = 3
    assert C == P and NSTEP % PRING == 0 and NT % 8 == 0
    assert CW == G4 * P and MAX_START % 2 == 0 and DIAG % 2 == 0

    def diag(t):
        c, j = STEPS[t]
        return j >= DIAG * c

    def width(t):
        c, j = STEPS[t]
        return CW - P * max(0, j - DIAG * c)

    def max_plan():
        work, load = [0], [0]
        for i, kc, heads, keys in CHUNKS:
            work.append(work[-1] + len(heads) * keys + P // 2)
        plan = [None] * NSTEP
        start = 0
        for k in range(0, NSTEP, 2):
            t = (MAX_START + k) % NSTEP
            load.append(load[-1] + 2 * CW + width(t) + width(t + 1))
        for k in range(0, NSTEP, 2):
            t = (MAX_START + k) % NSTEP
            end = min(range(NP1 + 1), key=lambda n: abs(work[n] * load[-1] - load[k // 2 + 1] * work[-1]))
            cut = [start + (end - start) * j // 6 for j in range(7)]
            places = [(2 if t >= MAX_START else 1, range(cut[j], cut[j + 1])) for j in range(6)]
            plan[t], plan[t + 1] = places[:2], places[2:]
            start = end
        return plan

    MAX_PLAN = max_plan()
    EARLY = max(r.stop for places in MAX_PLAN for ahead, r in places if ahead == 2)

    NDIAG = sum(diag(t) for t in range(NSTEP))

    with ExitStack() as ctx:
        def sb(name, shape, dt):
            return ctx.enter_context(nc.sbuf_tensor(name, shape, dt))

        def sem(name):
            return ctx.enter_context(nc.semaphore(name))

        def dram(name, shape, dt):
            return nc.dram_tensor(name, shape, dt, kind="Internal").ap()

        ps = ctx.enter_context(nc.psum_tensor("ps", [P, 8, 512], F32))

        x_sb = sb("x_sb", [P, NT, C], F32)
        z_sb = sb("z_sb", [P, NT, C], F32)
        zT = sb("zT", [P, N], F32)
        w1_sb = sb("w1_sb", [P, E, F + FK], F32)
        w2_sb = sb("w2_sb", [P, E, FK, C], F32)
        b2_rows = sb("b2_rows", [P, E * C], BF16)
        w_all = sb("w_all", [P, 4 * C], F32)
        wgate = sb("wgate", [P, E], F32)
        b_qkv = sb("b_qkv", [P, 3], F32)
        bv_all = sb("bv_all", [P, C], F32)
        bp_all = sb("bp_all", [P, C], F32)

        ident = sb("ident", [P, P], F32)
        ones_bf = sb("ones_bf", [P, P], BF16)
        before = sb("before", [P, P], BF16)
        causal = sb("causal", [P, P], BF16)
        ident_bf = sb("ident_bf", [P, P], BF16)
        rev = sb("rev", [P, E], F32)
        minus_half = sb("minus_half", [P, NT], F32)
        starts = sb("starts", [1, NS], F32)

        stats = sb("stats", [P, NT, 6], F32)
        lnw = sb("lnw", [P, 6, NT], F32)
        mean = sb("mean", [P, NT], F32)
        rstd = sb("rstd", [P, NT], F32)
        logit = sb("logit", [P, NT, E], F32)
        gtmp = sb("gtmp", [P, NT, E], F32)
        slot_of = sb("slot_of", [P, NT, E], F32)
        gexp = sb("gexp", [P, NT, E], F32)
        gmax = sb("gmax", [P, 3, NT], F32)
        score = sb("score", [P, NT], F32)
        onehot = sb("onehot", [P, NT, E], BF16)
        scanA = sb("scanA", [P, NT // 2 + NT, E], F32)
        scanB = sb("scanB", [P, NT // 2 + NT, E], F32)
        cnt_i = sb("cnt_i", [P, 2, E], I32)
        padA = sb("padA", [P, E // 2 + E], F32)
        padB = sb("padB", [P, E // 2 + E], F32)
        ebase = sb("ebase", [P, E], F32)
        pos_f = sb("pos_f", [P, NT], F32)
        pos = sb("pos", [P, NT], I32)
        ecmp = sb("ecmp", [1, NS, E - 1], F32)
        etab_f = sb("etab_f", [1, NS], F32)
        etab = sb("etab", [1, NS], I32)

        AW = 2 * (4 * 2 * T // 2) + 4 * QT * P + PRING * 4 * CW + 384
        arena = sb("arena", [P, AW], F32)

        def carve(at, words):
            assert at + words <= AW
            return arena[:, at:at + words], at + words

        gath, at = carve(0, NT * C)
        xin, at = carve(at, 4 * C)
        xs, at = carve(at, 2 * P)
        w1_now, at = carve(at, 2 * (F + FK))
        hT, at = carve(at, 2 * F)
        yr, at = carve(at, 4 * C)
        gath = gath.rearrange("p (a c) -> p a c", a=NT)
        xin = xin.rearrange("p (r c) -> p r c", r=4)
        xs = xs.rearrange("p (r c) -> p r c", r=2)
        w1_now = w1_now.rearrange("p (r c) -> p r c", r=2)
        hT = hT.rearrange("p (r k c) -> p r k c", r=2, k=FK)
        yr = yr.rearrange("p (r c) -> p r c", r=4)

        q_stk, at = carve(0, 4 * 2 * T // 2)
        k_stk, at = carve(at, 4 * 2 * T // 2)
        v_aug, at = carve(at, 4 * QT * P)
        prob, _ = carve(at, PRING * 4 * CW)
        vf, at = carve(at, 2 * CW)
        rf, at = carve(at, 2 * CW)
        parts, at = carve(at, 2 * 3 * CW)
        q_stk = q_stk.bitcast(BF16).rearrange("p (s r t) -> p s r t", s=4, r=2)
        k_stk = k_stk.bitcast(BF16).rearrange("p (s r t) -> p s r t", s=4, r=2)
        v_aug = v_aug.rearrange("p (s j h d) -> p s j h d", s=4, j=QT, h=4)
        prob = prob.rearrange("p (s g h n) -> p s g h n", s=PRING, g=2, h=2)
        vf = vf.rearrange("p (r n) -> p r n", r=2)
        rf = rf.rearrange("p (r n) -> p r n", r=2)
        parts = parts.bitcast(BF16).rearrange("p (b r s n) -> p b r s n", b=2, r=2, s=3)

        v_all = sb("v_all", [P, NT, C], F32)
        yraw = sb("yraw", [P, NCH, CW], F32)
        rden = sb("rden", [P, NCH, DIAG, 4], F32)
        mx = sb("mx", [P, 2, 4, QT], F32)
        mx0 = sb("mx0", [P, 4, QT], F32)
        nm = sb("nm", [4 * QT, 3, P], F32)
        nm_parts = sb("nm_parts", [4 * QT, 3, P], BF16)

        wattn_in, at = carve(at, 3 * C)
        la_in, at = carve(at, C)
        lb_in, at = carve(at, 3 * R)
        wproj_in, at = carve(at, C)
        lap_in, at = carve(at, C)
        lbp_in, at = carve(at, R)
        lbT, at = carve(at, 4 * C)
        wattn_in = wattn_in.rearrange("p (j c) -> p j c", j=3)
        lb_in = lb_in.rearrange("p (j r) -> p j r", j=3)
        la_in, lap_in, lbT = la_in[0:R], lap_in[0:R], lbT[0:R]
        wgred_in = sb("wgred_in", [GD, C], F32)
        wg_in = sb("wg_in", [E, GD], F32)
        wg_sq = sb("wg_sq", [E, GD], F32)
        wg_n = sb("wg_n", [E, 3], F32)
        wg_unit = sb("wg_unit", [E, GD], F32)
        wgT = sb("wgT", [GD, E], F32)
        b1_in = sb("b1_in", [E * FK, P], F32)
        BF_W = E * C // P
        bias_in = sb("bias_in", [P, BF_W], F32)
        bias_r = sb("bias_r", [P, 2, BF_W], F32)
        bias_parts = sb("bias_parts", [P, 3, BF_W], BF16)

        slots = dram("slots", [NS * P, C], F32)
        yslots = dram("yslots", [NS * P, C], F32)
        bias_d = dram("bias_d", [3, E * C], BF16)
        stack_d = dram("stack_d", [2, HEADS, SR, N], BF16)
        nm_d = dram("nm_d", [3, 4 * QT, P], BF16)
        x_dram = x.rearrange("b t c -> (b t) c").rearrange("(a p) c -> p a c", p=P)
        out_dram = out.rearrange("b t c -> (b t) c").rearrange("(a p) c -> p a c", p=P)

        block = ctx.enter_context(nc.Block())
        TILE_STEPS = NS + 2
        FIRST = 8
        LAST = FIRST + 4 * ((NS - FIRST) // 4)

        def tile_steps(eng, step):
            for s in range(FIRST):
                step(s, s % 4, s // 4)
            with eng.Fori(FIRST // 4, LAST // 4) as turn:
                for r in range(4):
                    step(turn * 4 + r, r, turn)
            for s in range(LAST, TILE_STEPS):
                step(s, s % 4, s // 4)

        def runs(s, lag):
            return not isinstance(s, int) or 0 <= s - lag < NS

        def later(s, lag):
            return not isinstance(s, int) or s - lag >= 0

        def per_ring(r):
            return (NS - r + 3) // 4

        x_in = [sem(f"x_in{g}") for g in range(4)]
        w1_in, w2_in, small_in, gate_in, bias_i, bias_out, bias_back = (
            sem(n) for n in ("w1_in", "w2_in", "small_in", "gate_in", "bias_i", "bias_out", "bias_back"))
        consts, zeros_done, slots_clear = sem("consts"), sem("zeros_done"), sem("slots_clear")
        CONSTS = 17
        bn_done, etab_done, root_in, root_done = sem("bn_done"), sem("etab_done"), sem("root_in"), sem("root_done")
        dve = sem("dve")
        wprep_pe, wprep_got = sem("wprep_pe"), sem("wprep_got")
        bias_split = sem("bias_split")
        z_ready, zt_put, zt_got = sem("z_ready"), sem("zt_put"), sem("zt_got")
        logits_done, gate_sub, gate_exp, onehot_done, counted, pos_done = (
            sem(n) for n in ("logits_done", "gate_sub", "gate_exp", "onehot_done", "counted", "pos_done"))
        scattered = sem("scattered")
        slot_in = [sem(f"slot_in{r}") for r in range(4)]
        xt_put, xt_got, w1_got, up_done, gelu_done, down_done, y_got = (
            sem(n) for n in ("xt_put", "xt_got", "w1_got", "up_done", "gelu_done", "down_done", "y_got"))
        y_out = [sem(f"y_out{r}") for r in range(4)]
        gathered = [sem(f"gathered{g}") for g in range(4)]
        moe_added, out_done = sem("moe_added"), sem("out_done")

        SMALL_LOADS = 9
        wt_put, wt_got = sem("wt_put"), sem("wt_got")
        qk_put, v32_got, hi_got, rest_got, mid_got, parts_done = (
            sem(n) for n in ("qk_put", "v32_got", "hi_got", "rest_got", "mid_got", "parts_done"))
        qk_out = [[sem(f"q_out{b}"), sem(f"k_out{b}")] for b in range(2)]
        v_mul, v_got, k_ones, v_ones = sem("v_mul"), sem("v_got"), sem("k_ones"), sem("v_ones")
        stack_in = [sem(f"stack_in{s}") for s in range(4)]
        quad_free, vaug_in = sem("quad_free"), sem("vaug_in")
        max_mul, max_free, max_done = sem("max_mul"), sem("max_free"), sem("max_done")
        nm_pool, nm_done, nm_out, nm_in = sem("nm_pool"), sem("nm_done"), sem("nm_out"), sem("nm_in")
        score_mul = [sem("score_mulA"), sem("score_mulB")]
        exp_done = [sem("exp_doneA"), sem("exp_doneB")]
        causal_done, prob_free, sums_got, turned, rden_done = (
            sem(n) for n in ("causal_done", "prob_free", "sums_got", "turned", "rden_done"))
        pv_free = [sem(f"pv_free{c}") for c in range(NCH)]
        yt_put, yt_got, proj_mul, proj_sum, bias_added = (
            sem(n) for n in ("yt_put", "yt_got", "proj_mul", "proj_sum", "bias_added"))
        passed_pool = sem("passed_pool")
        OUT_RUN = STACK_RUNS * DMA
        NQK = N // CW

        def quads(eng, quad):
            with eng.Fori(0, B - 1) as b:
                for r in range(QUADS):
                    quad(b, r, b * QUADS + r)
            for r in range(QUADS):
                quad(B - 1, r, (B - 1) * QUADS + r)

        BATCH_STEPS = QUADS * NSTEP

        def score_steps(eng, step, head, tail):
            def at(b, g):
                q, t = divmod(g, NSTEP)
                step(b, q, b * QUADS + q, t)
            for g in range(head):
                at(0, g)
            with eng.Fori(0, B - 1) as b:
                for g in range(head, head + BATCH_STEPS):
                    at(b, g)
            for g in range(head, BATCH_STEPS + tail):
                at(B - 1, g)

        def real(u):
            return not isinstance(u, int) or 0 <= u < NQ

        def first(u):
            return isinstance(u, int) and u == 0

        def chunk_item(u, n):
            return n if first(u) else u * MAX_ITEMS + (n - 1 + (n >= TURN_AT))

        def turn_item(u):
            return (u + 1) * MAX_ITEMS + (TURN_AT - 1 if real(u + 1) else -1)

        def chunk_bank(u, r, n):
            return 5 + (n if first(u) else r * MAX_ITEMS + n - 1 + (n >= TURN_AT)) % 2

        def turn_bank(u, r):
            return 5 + ((r + 1) * MAX_ITEMS + (TURN_AT if real(u + 1) else 0) - 1) % 2

        PV_BANK = (4, 7)

        def stored(eng, n):
            for b in range(2):
                for w in range(2):
                    eng.wait_ge(qk_out[b][w], n // 2 * OUT_RUN)

        def attention_sp(sp):
            rows = stack_d.rearrange("w h (d k) n -> w (h d) k n", d=HD)

            def store(n):
                for w in range(2):
                    sp.wait_ge(parts_done, n * 2 + (w + 1))
                    cols = slice(n * CW, (n + 1) * CW)
                    for k0, blocks, src in (((0, 3, parts[:, n % 2, w, 0:1, :].broadcast_to([P, 3, CW])),
                                             (3, 3, parts[:, n % 2, w, 1:2, :].broadcast_to([P, 3, CW])),
                                             (6, 1, parts[:, n % 2, w, 2:3, :])),
                                            ((0, 3, parts[:, n % 2, w, :, :]), (3, 3, parts[:, n % 2, w, :, :]), (6, 1, parts[:, n % 2, w, 0:1, :])))[w]:
                        sp.dma_start(rows[w, :, k0:k0 + blocks, cols], src).then_inc(qk_out[n % 2][w], DMA)

            def load_stack(b, r, u):
                sp.wait_ge(quad_free, u + 1)
                for w, stk in ((0, q_stk), (1, k_stk)):
                    for half in range(2):
                        src = stack_d[w, 4 * r + half:4 * r + half + 3:2, :, bass.ds(b * T, T)].rearrange("h s t -> s h t")
                        sp.dma_start(stk[64 * half:64 * half + SR, r, :, :], src).then_inc(stack_in[r], DMA)

            def pass_maxima(r, u):
                sp.wait_ge(nm_done, u + 1)
                if not isinstance(u, int) or u > 0:
                    sp.wait_ge(nm_in, u * 2 * DMA)
                sp.dma_start(nm_d.rearrange("s m q -> m s q"), nm_parts[:]).then_inc(nm_out, DMA)
                sp.wait_ge(nm_out, (u + 1) * DMA)
                rows = nm_d.rearrange("s (g h i) q -> h s g (i q)", g=2, h=2)
                for half in range(2):
                    sp.dma_start(q_stk[64 * half + SR:64 * half + KR, r, :, :], rows[half]).then_inc(nm_in, DMA)

            for n in range(NCH):
                store(n)
            stored(sp, NCH)
            sp.wait_ge(k_ones, 1)
            load_stack(0, 0, 0)
            load_stack(0, 1, 1)
            for n in range(NCH, NQK):
                store(n)
            stored(sp, NQK)
            pass_maxima(0, 0)

            def quad(b, r, u):
                if real(u + 2):
                    load_stack(b + (r + 2) // QUADS, (r + 2) % QUADS, u + 2)
                if real(u + 1):
                    pass_maxima((r + 1) % QUADS, u + 1)
            quads(sp, quad)

        def attention_pool(pool):
            pool.wait_ge(moe_added, NT)
            pool.memset(k_stk[:], 1.0).then_inc(k_ones, 1)

            pool.wait_ge(z_ready, 2 * NG)
            for g in range(NG):
                for w in range(2):
                    pool.wait_ge(mid_got, g * 2 + (w + 1))
                    pool.tensor_tensor(parts[:, g % 2, w, 2, :], rf[:, w, :], parts[:, g % 2, w, 1, :], ALU.subtract).then_inc(parts_done, 1)
                xg = x_sb[:, G4 * g:G4 * (g + 1), :]
                pool.tensor_tensor(xg, xg, bp_all[:].unsqueeze(1).broadcast_to([P, G4, C]), ALU.add).then_inc(bias_added, 1)
            pool.wait_ge(v_got, NG)
            pool.wait_ge(v_ones, 1)

            def values(b, r, u):
                pool.wait_ge(quad_free, u + 1)
                pool.sem_inc(passed_pool, 1)
                pool.tensor_copy(v_aug[:, r, :, :, 0:HD],
                                 v_all[:, bass.ds(b * QT, QT), r * 4 * HD:(r + 1) * 4 * HD].rearrange("p j (h d) -> p j h d", h=4)).then_inc(vaug_in, 1)
            values(0, 0, 0)

            def split_maxima(u):
                pool.wait_ge(max_free, turn_item(u) + 3)
                if not first(u):
                    pool.wait_ge(nm_out, u * DMA)
                pool.sem_inc(passed_pool, 1)
                pool.tensor_copy(nm_parts[:, 0, :], nm[:, 0, :]).then_inc(nm_pool, 1)
                pool.wait_ge(nm_pool, u * 3 + 1)
                pool.tensor_tensor(nm[:, 1, :], nm[:, 0, :], nm_parts[:, 0, :], ALU.subtract).then_inc(nm_pool, 1)
                pool.wait_ge(nm_pool, u * 3 + 2)
                pool.sem_inc(passed_pool, 1)
                pool.tensor_copy(nm_parts[:, 1, :], nm[:, 1, :]).then_inc(nm_pool, 1)
                pool.wait_ge(nm_pool, u * 3 + 3)
                pool.tensor_tensor(nm_parts[:, 2, :], nm[:, 1, :], nm_parts[:, 1, :], ALU.subtract).then_inc(nm_done, 1)

            split_maxima(0)

            def quad(b, r, u):
                if real(u + 1):
                    values(b + (r + 1) // QUADS, (r + 1) % QUADS, u + 1)
                for t in range(NSTEP):
                    if t == MAX_START and real(u + 1):
                        split_maxima(u + 1)
                    if diag(t):
                        for g in range(2):
                            pool.wait_ge(exp_done[g], u * NSTEP + (t + 1))
                            pool.sem_inc(passed_pool, 1)
                            tri = prob[:, t % PRING, g, :, 0:P]
                            pool.affine_select(out=tri, in_=tri, compare_op=ALU.is_ge, fill=0.0, base=0,
                                               pattern=[[0, 2], [1, P]], channel_multiplier=-1).then_inc(causal_done, 1)
            quads(pool, quad)

        def attention_act(act):
            act.wait_ge(small_in, SMALL_LOADS * DMA)

            for n in range(NQK):
                for w in range(2):
                    act.wait_ge(qk_put, n * 2 + (w + 1))
                    if n > 0:
                        act.wait_ge(rest_got, n * 2 + (w - 1))
                    act.activation(vf[:, w, :], ps[:, 2 + w, :], ACT.Identity, bias=b_qkv[:, w:w + 1]).then_inc(v32_got, 1)
                    act.wait_ge(v32_got, n * 2 + (w + 1))
                    if n > 1:
                        act.wait_ge(qk_out[n % 2][w], n // 2 * OUT_RUN)
                    act.copy(parts[:, n % 2, w, 0, :], vf[:, w, :]).then_inc(hi_got, 1)
                for w in range(2):
                    act.wait_ge(rest_got, n * 2 + (w + 1))
                    act.copy(parts[:, n % 2, w, 1, :], rf[:, w, :]).then_inc(mid_got, 1)
            stored(act, NQK)

            def take_sums(u, c):
                act.wait_ge(prob_free, u * NSTEP + (PRING + (DIAG, NSTEP)[c]))
                act.copy(yraw[:, c, :], ps[:, PV_BANK[c], :]).then_inc(sums_got, 1)

            def step(b, q, u, t):
                n = width(t)
                if real(u):
                    for g in range(2):
                        act.wait_ge(score_mul[g], u * NSTEP + (t + 1))
                        act.wait_ge(prob_free, u * NSTEP + (t + 1))
                        act.activation(prob[:, t % PRING, g, :, 0:n], ps[:, 2 * g:2 * g + 2, 0:n], ACT.Exp,
                                       scale=SCALE).then_inc(exp_done[g], 1)
                if t == 0 and real(u - 1):
                    take_sums(u - 1, 1)
                if t == DIAG and real(u):
                    take_sums(u, 0)
            score_steps(act, step, 2, 2)

            for g in range(NG):
                act.wait_ge(yt_put, g + 1)
                act.copy(zT[:, g * 512:(g + 1) * 512], ps[:, g % 2, :]).then_inc(yt_got, 1)

        def prepare_attention(v, put, own):
            v.wait_ge(wt_put, 1)
            put(v.tensor_copy(w_all[:], ps[:, 6, :]))
            v.tensor_copy(lbT[:], ps[0:R, 7, :]).then_inc(wt_got, 1)
            v.wait_ge(wt_put, 2)
            own()
            v.scalar_tensor_tensor(out=w_all[:], in0=ps[:, 6, :], scalar=LORA_SCALE, in1=w_all[:],
                                   op0=ALU.mult, op1=ALU.add).then_inc(wt_got, 1)

        def take_values(v, half):
            for g in range(2 * half, 2 * half + 2):
                v.wait_ge(v_mul, g + 1)
                v.tensor_tensor(v_all[:, G4 * g:G4 * (g + 1), :], ps[:, 4 + g % 2, :].rearrange("p (a c) -> p a c", a=G4),
                                bv_all[:].unsqueeze(1).broadcast_to([P, G4, C]), ALU.add).then_inc(v_got, 1)

        def attention_dve(v, moments, normalise):
            def qk_rest(n):
                for w in range(2):
                    v.wait_ge(hi_got, n * 2 + (w + 1))
                    if n > 0:
                        v.wait_ge(parts_done, n * 2 + (w - 1))
                    v.tensor_tensor(rf[:, w, :], vf[:, w, :], parts[:, n % 2, w, 0, :], ALU.subtract).then_inc(rest_got, 1)

            def join_maxima(u, r):
                v.wait_ge(max_free, chunk_item(u, NP1 - 1) + 3)
                both = mx[:, r % 2, :, DIAG:]
                v.tensor_tensor(both, both, mx0[:, :, DIAG:], ALU.max).then_inc(max_done, 1)

            def negate_maxima(u, r):
                if not first(u):
                    v.wait_ge(nm_done, u)
                v.wait_ge(max_mul, turn_item(u) + 1)
                v.tensor_scalar(nm[:, 0, :], ps[0:4 * QT, turn_bank(u, r), 0:P], -1.0, None, ALU.mult).then_inc(max_free, 1)

            def maxima(u, r, chunks):
                for n in chunks:
                    if n == TURN_AT and not first(u):
                        negate_maxima(u - 1, r - 1)
                    i, kc, heads, keys = CHUNKS[n]
                    item = chunk_item(u, n)
                    v.wait_ge(max_mul, item + 1)
                    bank = ps[:, chunk_bank(u, r, n), 0:len(heads) * keys].rearrange("p (h k) -> p h k", k=keys)
                    to = mx[:, r % 2, :, :] if kc == i // DIAG else mx0[:]
                    v.tensor_reduce(to[:, heads[0]:heads[-1] + 1:2, i], bank, AX_X, ALU.max).then_inc(max_free, 1)

            def divide(b, q, u, c):
                r = q % QUADS
                v.wait_ge(turned, u * NCH + (c + 1))
                sums = ps[:, PV_BANK[c], :].rearrange("p (a h d) -> p a h d", a=DIAG, h=4)
                v.reciprocal(rden[:, c], sums[:, :, :, HD]).then_inc(rden_done, 1)
                v.wait_ge(rden_done, u * NCH + (c + 1))
                t0 = (b + (q - r) // QUADS) * QT + DIAG * c
                v.tensor_tensor(z_sb[:, bass.ds(t0, DIAG), r * 4 * HD:(r + 1) * 4 * HD].rearrange("p a (h d) -> p a h d", h=4),
                                sums[:, :, :, 0:HD], rden[:, c].unsqueeze(3).broadcast_to([P, DIAG, 4, HD]), ALU.mult).then_inc(pv_free[c], 1)

            for n in range(NCH):
                qk_rest(n)
            share = [k * NP1 // (NQK - NCH) for k in range(NQK - NCH + 1)]
            for n in range(NCH, NQK):
                qk_rest(n)
                maxima(0, 0, range(share[n - NCH], share[n - NCH + 1]))
            join_maxima(0, 0)
            maxima(1, 1, range(EARLY))

            def step(b, q, u, t):
                if t == MAX_START and real(u + 1) and not real(u + 2):
                    negate_maxima(u + 1, q + 1)
                for ahead, chunks in MAX_PLAN[t]:
                    if real(u + ahead):
                        maxima(u + ahead, q + ahead, chunks)
                        if NP1 - 1 in chunks:
                            join_maxima(u + ahead, q + ahead)
                if t == 2 and real(u - 1):
                    divide(b, q - 1, u - 1, 1)
                if t == DIAG + 2 and real(u):
                    divide(b, q, u, 0)
            score_steps(v, step, 4, 4)

            v.wait_ge(bias_added, NG)
            for g in range(NG):
                v.wait_ge(proj_mul, g + 1)
                xg = x_sb[:, G4 * g:G4 * (g + 1), :]
                v.tensor_tensor(xg, ps[:, 2 + g % 2, :].rearrange("p (a c) -> p a c", a=G4), xg, ALU.add).then_inc(proj_sum, 1)
                if g % 2:
                    v.wait_ge(proj_sum, g + 1)
                    moments(2, g // 2)
                    if g > 1:
                        normalise(2, g // 2 - 1)

        def attention_pe_weights(pe):
            pe.wait_ge(small_in, SMALL_LOADS * DMA)
            pe.wait_ge(y_got, NS)
            for j in range(3):
                pe.transpose(ps[:, 6, j * P:(j + 1) * P], wattn_in[:, j, :], ident[:])
                pe.transpose(ps[0:R, 7, j * P:(j + 1) * P], lb_in[:, j, :], ident[:])
            pe.transpose(ps[:, 6, 3 * P:4 * P], wproj_in[:], ident[:])
            pe.transpose(ps[0:R, 7, 3 * P:4 * P], lbp_in[:], ident[:]).then_inc(wt_put, 1)
            pe.wait_ge(wt_got, 1)
            pe.matmul(ps[:, 6, 0:3 * C], la_in[:], lbT[:, 0:3 * C], start=True, stop=True)
            pe.matmul(ps[:, 6, 3 * C:], lap_in[:], lbT[:, 3 * C:], start=True, stop=True).then_inc(wt_put, 1)

        def attention_pe(pe):
            pe.wait_ge(wt_got, 2)
            pe.sem_inc(quad_free, 4)
            pe.sem_inc(max_free, 2)
            for c in range(NCH):
                pe.sem_inc(pv_free[c], 1)
            pe.sem_inc(prob_free, PRING)

            def value(g):
                pe.wait_ge(zt_got, NG + g + 1)
                if g >= 2:
                    pe.wait_ge(v_got, g - 1)
                for a in range(G4):
                    t = G4 * g + a
                    mm = pe.matmul(ps[:, 4 + g % 2, a * C:(a + 1) * C], zT[:, t * P:(t + 1) * P], w_all[:, 2 * C:3 * C], start=True, stop=True)
                mm.then_inc(v_mul, 1)

            for g in transposes(pe, 1):
                if g >= 2:
                    value(g - 2)
            value(NG - 2)
            value(NG - 1)

            def project(n):
                for w in range(2):
                    if n > 0:
                        pe.wait_ge(v32_got, n * 2 + (w - 1))
                    pe.matmul(ps[:, 2 + w, :], w_all[:, w * C:(w + 1) * C], zT[:, n * CW:(n + 1) * CW], start=True, stop=True).then_inc(qk_put, 1)

            def turn_maxima(u, r):
                pe.wait_ge(max_done, u + 1)
                pe.wait_ge(max_free, turn_item(u) + 1)
                pe.transpose(ps[0:4 * QT, turn_bank(u, r), 0:P], mx[:, r % 2, :, :].rearrange("p h i -> p (h i)"),
                             ident[:]).then_inc(max_mul, 1)

            def max_scores(u, r, chunks):
                for n in chunks:
                    if n == TURN_AT and not first(u):
                        turn_maxima(u - 1, r - 1)
                    i, kc, heads, keys = CHUNKS[n]
                    bank = chunk_bank(u, r, n)
                    diagonal = kc == i // DIAG
                    pe.wait_ge(max_free, chunk_item(u, n) + 1)
                    for at, h in enumerate(heads):
                        pr, hh = divmod(h, 2)
                        rows = slice(64 * hh, 64 * hh + SR)
                        mm = pe.matmul(ps[:, bank, at * keys:(at + 1) * keys], q_stk[rows, r % QUADS, pr, i * P:(i + 1) * P],
                                       k_stk[rows, r % QUADS, pr, kc * 512:kc * 512 + keys], start=True, stop=not diagonal)
                        if diagonal:
                            mm = pe.matmul(ps[:, bank, (at + 1) * keys - P:(at + 1) * keys], ident_bf[:], causal[:], start=False, stop=True)
                    mm.then_inc(max_mul, 1)

            def scores(u, r, t, g):
                c, j = STEPS[t]
                n = width(t)
                if t == 0 and g == 0:
                    pe.wait_ge(nm_in, (u + 1) * 2 * DMA)
                if not (isinstance(u, int) and u == 0 and t == 0):
                    pe.wait_ge(exp_done[g], u * NSTEP + t)
                for hh in range(2):
                    rows = slice(64 * hh, 64 * hh + KR)
                    mm = pe.matmul(ps[:, 2 * g + hh, 0:n], k_stk[rows, r, g, j * P:(j + 1) * P],
                                   q_stk[rows, r, g, (c + 1) * CW - n:(c + 1) * CW], start=True, stop=True)
                mm.then_inc(score_mul[g], 1)

            def weigh(u, r, t):
                c, j = STEPS[t]
                n = width(t)
                for g in range(2):
                    pe.wait_ge(exp_done[g], u * NSTEP + (t + 1))
                if diag(t):
                    d = sum(diag(s) for s in range(t + 1))
                    pe.wait_ge(causal_done, u * 2 * NDIAG + 2 * d)
                if t == 0:
                    pe.wait_ge(vaug_in, u + 1)
                if j == 0:
                    pe.wait_ge(pv_free[c], u + 1)
                for h in range(4):
                    mm = pe.matmul(ps[32 * h:32 * h + 32, PV_BANK[c], CW - n:CW], v_aug[:, r, j, h, :],
                                   prob[:, t % PRING, h // 2, h % 2, 0:n], start=(j == 0), stop=(j == DIAG * (c + 1) - 1))
                mm.then_inc(prob_free, 1)

            def turn_out(u, c):
                pe.wait_ge(sums_got, u * NCH + (c + 1))
                for a in range(DIAG):
                    mm = pe.transpose(ps[:, PV_BANK[c], a * P:(a + 1) * P], yraw[:, c, a * P:(a + 1) * P], ident[:])
                    if c == NCH - 1 and a == 0:
                        mm.then_inc(quad_free, 1)
                mm.then_inc(turned, 1)

            share = [k * NP1 // (NQK - NCH) for k in range(NQK - NCH + 1)]
            project(0)
            for n in range(NQK):
                if n + 1 < NQK:
                    project(n + 1)
                if n == NCH:
                    pe.wait_ge(v_got, NG)
                    pe.wait_ge(stack_in[0], 4 * DMA)
                if n >= NCH:
                    max_scores(0, 0, range(share[n - NCH], share[n - NCH + 1]))
            pe.wait_ge(v32_got, 2 * NQK)
            pe.wait_ge(stack_in[1], 4 * DMA)
            max_scores(1, 1, range(EARLY))
            for g in range(2):
                scores(0, 0, 0, g)

            def step(b, q, u, t):
                nq, nt = divmod(q * NSTEP + t + 1, NSTEP)
                nu = u + (nq - q)
                if t == MAX_START and real(u + 2):
                    pe.wait_ge(stack_in[(q + 2) % QUADS], (b + ((q + 2) // QUADS + 1)) * 4 * DMA)

                def some_max(place):
                    ahead, chunks = MAX_PLAN[t][place]
                    if real(u + ahead):
                        max_scores(u + ahead, q + ahead, chunks)

                if t == MAX_START and real(u + 1) and not real(u + 2):
                    turn_maxima(u + 1, q + 1)
                for g in range(2):
                    if real(nu):
                        scores(nu, nq % QUADS, nt, g)
                    some_max(g)
                if t % 2:
                    for late in (1, 0):
                        if real(u):
                            weigh(u, q % QUADS, t - late)
                        some_max(3 - late)
                if t == 1 and real(u - 1):
                    turn_out(u - 1, 1)
                if t == DIAG + 1 and real(u):
                    turn_out(u, 0)
            score_steps(pe, step, 2, 2)

            def proj(g):
                pe.wait_ge(yt_got, g + 1)
                if g >= 2:
                    pe.wait_ge(proj_sum, g - 1)
                for a in range(G4):
                    t = G4 * g + a
                    mm = pe.matmul(ps[:, 2 + g % 2, a * C:(a + 1) * C], zT[:, t * P:(t + 1) * P], w_all[:, 3 * C:], start=True, stop=True)
                mm.then_inc(proj_mul, 1)
            for c in range(NCH):
                pe.wait_ge(pv_free[c], NQ + 1)
            for g in range(NG):
                if g >= 2:
                    pe.wait_ge(yt_got, g - 1)
                for a in range(G4):
                    mm = pe.transpose(ps[:, g % 2, a * P:(a + 1) * P], z_sb[:, G4 * g + a, :], ident[:])
                mm.then_inc(yt_put, 1)
                if g >= 1:
                    proj(g - 1)
            proj(NG - 1)

        def transposes(pe, n):
            for g in range(NG):
                pe.wait_ge(z_ready, NG * n + g + 1)
                if g >= 2:
                    pe.wait_ge(zt_got, NG * n + g - 1)
                for a in range(G4):
                    mm = pe.transpose(ps[:, g % 2, a * P:(a + 1) * P], z_sb[:, G4 * g + a, :], ident[:])
                mm.then_inc(zt_put, 1)
                yield g

        def take_transposes(act, n):
            for g in range(NG):
                act.wait_ge(zt_put, NG * n + g + 1)
                act.copy(zT[:, g * 512:(g + 1) * 512], ps[:, g % 2, :]).then_inc(zt_got, 1)

        @block.sync
        def _(sp):
            sp.dma_start(x_sb[:, 0:8, :], x_dram[:, 0:8, :]).then_inc(x_in[0], DMA)
            sp.dma_start(wg_in[:], wg).then_inc(gate_in, DMA)
            sp.dma_start(wgred_in[:], wg_red).then_inc(gate_in, DMA)
            for g in range(1, 4):
                sp.dma_start(x_sb[:, 8 * g:8 * g + 8, :], x_dram[:, 8 * g:8 * g + 8, :]).then_inc(x_in[g], DMA)
            sp.dma_start(b1_in[:], b1.rearrange("e (k p) -> (e k) p", p=P)).then_inc(bias_i, DMA)
            sp.dma_start(bias_in[:], b2.rearrange("e f -> (e f)").rearrange("(p n) -> p n", p=P)).then_inc(bias_i, DMA)
            sp.wait_ge(zeros_done, 1)
            sp.dma_start(slots.rearrange("(j p) c -> p j c", p=P), gath[:, 0:1, :].broadcast_to([P, NS, C])).then_inc(slots_clear, DMA)
            sp.dma_start(w1_sb[:, :, 0:F], w1.rearrange("e c f -> c e f")).then_inc(w1_in, DMA)
            sp.dma_start(w2_sb[:], w2.rearrange("e (k p) c -> p e k c", p=P)).then_inc(w2_in, DMA)
            sp.wait_ge(bias_split, 1)
            for k in range(3):
                sp.dma_start(bias_d[k].rearrange("(p n) -> p n", p=P), bias_parts[:, k, :]).then_inc(bias_out, DMA)
            sp.wait_ge(bias_out, 3 * DMA)
            sp.wait_ge(consts, CONSTS)
            sp.dma_start(b2_rows[0:3, :], bias_d).then_inc(bias_back, DMA)
            sp.dma_start(wattn_in[:], w_attn.rearrange("(j p) c -> p j c", p=P)).then_inc(small_in, DMA)
            sp.dma_start(la_in[:], la_attn).then_inc(small_in, DMA)
            sp.dma_start(lb_in[:], lb_attn.rearrange("(j p) r -> p j r", p=P)).then_inc(small_in, DMA)
            sp.dma_start(wproj_in[:], w_proj).then_inc(small_in, DMA)
            sp.dma_start(lap_in[:], la_proj).then_inc(small_in, DMA)
            sp.dma_start(lbp_in[:], lb_proj).then_inc(small_in, DMA)
            with nc.allow_non_contiguous_dma(reason="three bias values per partition"):
                sp.dma_start(b_qkv[:], b_attn.rearrange("(j p) -> p j", p=P)).then_inc(small_in, DMA)
            sp.dma_start(bv_all[:], b_attn[2 * C:].rearrange("(o c) -> o c", o=1).broadcast_to([P, C])).then_inc(small_in, DMA)
            sp.dma_start(bp_all[:], b_proj.rearrange("(o c) -> o c", o=1).broadcast_to([P, C])).then_inc(small_in, DMA)

            def moe(f):
                def step(s, r, turn):
                    if not runs(s, 0):
                        return
                    if later(s, 4):
                        sp.wait_ge(xt_put, s + (f * NS - 3))
                    sp.dma_start(xin[:, r, :], slots[bass.ds(s * P, P), :]).then_inc(slot_in[r], DMA)
                sp.wait_ge(scattered, (f + 1) * NT * DMA)
                tile_steps(sp, step)

            moe(0)
            attention_sp(sp)
            moe(1)
            for g in range(4):
                sp.wait_ge(moe_added, NT + 8 * (g + 1))
                sp.dma_start(out_dram[:, 8 * g:8 * g + 8, :], x_sb[:, 8 * g:8 * g + 8, :]).then_inc(out_done, DMA)
            sp.wait_ge(out_done, 4 * DMA)

        @block.gpsimd
        def _(pool):
            pool.memset(gath[:, 0, :], 0.0).then_inc(zeros_done, 1)
            pool.memset(ident[:], 0.0).then_inc(consts, 1)
            pool.memset(ident_bf[:], 0.0).then_inc(consts, 1)
            pool.memset(ones_bf[:], 1.0).then_inc(consts, 1)
            pool.memset(before[:], 1.0).then_inc(consts, 1)
            pool.memset(causal[:], 0.0).then_inc(consts, 1)
            pool.memset(scanA[:], 0.0).then_inc(consts, 1)
            pool.memset(scanB[:], 0.0).then_inc(consts, 1)
            pool.memset(padA[:], 0.0).then_inc(consts, 1)
            pool.memset(padB[:], 0.0).then_inc(consts, 1)
            pool.memset(b2_rows[:].bitcast(F32), 0.0).then_inc(consts, 1)
            pool.memset(minus_half[:], -0.5).then_inc(consts, 1)
            pool.iota(rev[:], [[-1, E]], base=E, channel_multiplier=0, allow_small_or_imprecise_dtypes=True).then_inc(consts, 1)
            pool.iota(starts[:], [[P, NS]], base=0, channel_multiplier=0, allow_small_or_imprecise_dtypes=True).then_inc(consts, 1)
            pool.wait_ge(consts, CONSTS - 4)
            pool.affine_select(out=ident[:], in_=ident[:], compare_op=ALU.not_equal, fill=1.0, base=0,
                               pattern=[[-1, P]], channel_multiplier=1).then_inc(consts, 1)
            pool.affine_select(out=before[:], in_=before[:], compare_op=ALU.is_gt, fill=0.0, base=0,
                               pattern=[[1, P]], channel_multiplier=-1).then_inc(consts, 1)
            pool.affine_select(out=ident_bf[:], in_=ident_bf[:], compare_op=ALU.not_equal, fill=1.0, base=0,
                               pattern=[[-1, P]], channel_multiplier=1).then_inc(consts, 1)
            pool.affine_select(out=causal[:], in_=causal[:], compare_op=ALU.is_ge, fill=LOWEST, base=0,
                               pattern=[[-1, P]], channel_multiplier=1).then_inc(consts, 1)

            def deviation(n, g):
                pool.wait_ge(root_in, 4 * n + g + 2)
                pool.tensor_tensor(rstd[:, 8 * g:8 * g + 8], lnw[:, 5, 8 * g:8 * g + 8], minus_half[:, 0:8], ALU.pow).then_inc(root_done, 1)

            def moe(f):
                pool.wait_ge(pos_done, f + 1)
                if f == 0:
                    pool.wait_ge(slots_clear, DMA)
                for a in range(NT):
                    pool.indirect_dma_start(
                        out=slots, out_offset=bass.IndirectOffsetOnAxis(ap=pos[:, a:a + 1].bitcast(U32), axis=0),
                        in_=z_sb[:, a, :], in_offset=None, bounds_check=NS * P - 1).then_inc(scattered, DMA)
                for r in range(4):
                    pool.wait_ge(y_out[r], (f + 1) * per_ring(r) * DMA)
                for a in range(NT):
                    pool.indirect_dma_start(
                        out=gath[:, a, :], out_offset=None, in_=yslots,
                        in_offset=bass.IndirectOffsetOnAxis(ap=pos[:, a:a + 1].bitcast(U32), axis=0),
                        bounds_check=NS * P - 1).then_inc(gathered[a // 8], DMA)
                    if f == 0 and a % 8 == 7 and a > 8:
                        deviation(1, a // 8 - 1)
                if f == 0:
                    deviation(1, 3)

            pool.wait_ge(root_in, 1)
            pool.tensor_tensor(wg_n[:, 1:2], wg_n[:, 0:1], minus_half[0:E, 0:1], ALU.pow).then_inc(root_done, 1)
            for g in range(4):
                deviation(0, g)
            pool.memset(v_aug[:], 1.0).then_inc(v_ones, 1)
            moe(0)
            attention_pool(pool)
            for g in range(4):
                deviation(2, g)
            moe(1)

        @block.vector
        def _(v):
            n_dve = [0]

            def put(ins):
                n_dve[0] += 1
                ins.then_inc(dve, 1)

            def own():
                v.wait_ge(dve, n_dve[0])

            def square_gate():
                v.wait_ge(gate_in, 2 * DMA)
                v.tensor_tensor_reduce(out=wg_sq[:], in0=wg_in[:], in1=wg_in[:], scale=1.0, scalar=0.0,
                                       op0=ALU.mult, op1=ALU.add, accum_out=wg_n[:, 0:1]).then_inc(root_in, 1)

            def prepare():
                v.wait_ge(root_done, 1)
                put(v.tensor_scalar(wg_n[:, 2:3], wg_n[:, 1:2], 1.0 / NORM_EPS, None, ALU.min))
                own()
                v.tensor_scalar(wg_unit[:], wg_in[:], wg_n[:, 2:3], None, ALU.mult).then_inc(gate_sub, 1)
                v.wait_ge(bias_i, 2 * DMA)
                put(v.tensor_copy(bias_parts[:, 0, :], bias_in[:]))
                own()
                put(v.tensor_tensor(bias_r[:, 0, :], bias_in[:], bias_parts[:, 0, :], ALU.subtract))
                own()
                put(v.tensor_copy(bias_parts[:, 1, :], bias_r[:, 0, :]))
                own()
                v.tensor_tensor(bias_parts[:, 2, :], bias_r[:, 0, :], bias_parts[:, 1, :], ALU.subtract).then_inc(bias_split, 1)
                v.wait_ge(wprep_pe, 1)
                v.tensor_copy(wgT[:], ps[0:GD, 2, 0:E]).then_inc(wprep_got, 1)
                v.wait_ge(wprep_pe, 2)
                v.tensor_copy(wgate[:], ps[:, 2, 0:E]).then_inc(wprep_got, 1)
                v.wait_ge(wprep_pe, 3)
                v.tensor_copy(w1_sb[:, :, F:], ps[:, 2, 0:E * FK].rearrange("p (e k) -> p e k", e=E)).then_inc(wprep_got, 1)

            def moments(n, g):
                G = slice(8 * g, 8 * g + 8)
                for a in range(8 * g, 8 * g + 8):
                    last = v.bn_stats(stats[:, a, :], x_sb[:, a, :])
                last.then_inc(bn_done, 1)
                v.wait_ge(bn_done, 4 * n + g + 1)
                me, mo, qe, qo = (stats[:, G, k] for k in (1, 4, 2, 5))
                put(v.tensor_tensor(lnw[:, 0, G], me, mo, ALU.add))
                put(v.tensor_tensor(lnw[:, 1, G], me, mo, ALU.subtract))
                put(v.tensor_tensor(lnw[:, 2, G], qe, qo, ALU.add))
                own()
                put(v.tensor_scalar(mean[:, G], lnw[:, 0, G], 0.5, None, ALU.mult))
                put(v.tensor_tensor(lnw[:, 3, G], lnw[:, 1, G], lnw[:, 1, G], ALU.mult))
                put(v.tensor_scalar(lnw[:, 4, G], lnw[:, 2, G], 1.0 / C, LN_EPS, ALU.mult, ALU.add))
                own()
                v.scalar_tensor_tensor(out=lnw[:, 5, G], in0=lnw[:, 3, G], scalar=0.25, in1=lnw[:, 4, G],
                                       op0=ALU.mult, op1=ALU.add).then_inc(root_in, 1)

            def normalise(n, g):
                v.wait_ge(root_done, 4 * n + g + 2)
                for a in range(8 * g, 8 * g + 8):
                    z = v.tensor_scalar(z_sb[:, a, :], x_sb[:, a, :], mean[:, a:a + 1], rstd[:, a:a + 1], ALU.subtract, ALU.mult)
                    if a % G4 == G4 - 1:
                        z.then_inc(z_ready, 1)

            def over_e(t):
                return t.unsqueeze(2).broadcast_to([P, NT, E])

            def route(f):
                v.wait_ge(logits_done, f + 1)
                put(v.tensor_copy(logit[:], ps[:, 7, 0:NT * E].rearrange("p (a e) -> p a e", e=E)))
                own()
                put(v.tensor_reduce(gmax[:, 0, :], logit[:], AX_X, ALU.max))
                own()
                v.tensor_tensor(gtmp[:], logit[:], over_e(gmax[:, 0, :]), ALU.subtract).then_inc(gate_sub, 1)
                put(v.tensor_tensor(logit[:], logit[:], over_e(gmax[:, 0, :]), ALU.is_equal))
                own()
                put(v.tensor_tensor(logit[:], logit[:], rev[:].unsqueeze(1).broadcast_to([P, NT, E]), ALU.mult))
                own()
                put(v.tensor_reduce(gmax[:, 1, :], logit[:], AX_X, ALU.max))
                own()
                v.tensor_tensor(onehot[:], logit[:], over_e(gmax[:, 1, :]), ALU.is_equal).then_inc(onehot_done, 1)
                v.wait_ge(gate_exp, f + 1)
                put(v.tensor_reduce(gmax[:, 2, :], gexp[:], AX_X, ALU.add))
                own()
                put(v.reciprocal(score[:], gmax[:, 2, :]))
                own()
                put(v.tensor_scalar(score[:], score[:], BRANCH, None, ALU.mult))
                v.wait_ge(counted, f + 1)
                H = NT // 2
                tot = ps[:, 6, NT * E:2 * NT * E].rearrange("p (a e) -> p a e", e=E)
                front = ps[:, 6, 0:NT * E].rearrange("p (a e) -> p a e", e=E)
                put(v.tensor_copy(scanA[:, H:, :], tot))
                own()
                src, dst, d = scanA, scanB, 1
                while d < NT:
                    put(v.tensor_tensor(dst[:, H:, :], src[:, H:, :], src[:, H - d:H + NT - d, :], ALU.add))
                    own()
                    src, dst, d = dst, src, 2 * d
                put(v.tensor_scalar(cnt_i[:, 0, :], src[:, H + NT - 1, :], float(P - 1), None, ALU.add))
                own()
                SH = P.bit_length() - 1
                put(v.tensor_scalar(cnt_i[:, 1, :], cnt_i[:, 0, :], SH, SH, ALU.logical_shift_right, ALU.logical_shift_left))
                own()
                put(v.tensor_copy(padA[:, E // 2:], cnt_i[:, 1, :]))
                own()
                put(v.tensor_scalar(ebase[:], padA[:, E // 2:], -1.0, None, ALU.mult))
                a, b, d = padA, padB, 1
                while d < E:
                    put(v.tensor_tensor(b[:, E // 2:], a[:, E // 2:], a[:, E // 2 - d:E // 2 + E - d], ALU.add))
                    own()
                    a, b, d = b, a, 2 * d
                ends = a[:, E // 2:]
                put(v.tensor_tensor(ebase[:], ebase[:], ends, ALU.add))
                put(v.tensor_tensor(slot_of[:], src[:, H:, :], tot, ALU.subtract))
                own()
                put(v.tensor_tensor(slot_of[:], slot_of[:], front, ALU.add))
                own()
                put(v.tensor_tensor(slot_of[:], slot_of[:], ebase[:].unsqueeze(1).broadcast_to([P, NT, E]), ALU.add))
                own()
                put(v.tensor_tensor(slot_of[:], slot_of[:], onehot[:], ALU.mult))
                own()
                put(v.tensor_reduce(pos_f[:], slot_of[:], AX_X, ALU.add))
                own()
                v.tensor_copy(pos[:], pos_f[:]).then_inc(pos_done, 1)
                put(v.tensor_tensor(ecmp[:], starts[:].unsqueeze(2).broadcast_to([1, NS, E - 1]),
                                    ends[0:1, 0:E - 1].unsqueeze(1).broadcast_to([1, NS, E - 1]), ALU.is_ge))
                own()
                put(v.tensor_reduce(etab_f[:], ecmp[:], AX_X, ALU.add))
                own()
                v.tensor_copy(etab[:], etab_f[:]).then_inc(etab_done, 1)

            def experts(f):
                base = f * NS

                v.wait_ge(etab_done, f + 1)
                if f == 0:
                    v.wait_ge(w1_in, DMA)
                    v.wait_ge(wprep_got, 3)

                def step(s, r, turn):
                    if runs(s, 0):
                        e = v.value_load(etab[0:1, bass.ds(s, 1)], min_val=0, max_val=E - 1)
                        if later(s, 2):
                            v.wait_ge(gelu_done, s + (base - 1))
                        v.tensor_copy(w1_now[:, r % 2, :], w1_sb[:, bass.ds(e, 1), :].rearrange("p e f -> p (e f)")).then_inc(w1_got, 1)
                        v.wait_ge(xt_put, s + (base + 1))
                        v.tensor_copy(xs[:, r % 2, :], ps[:, r % 2, 0:P]).then_inc(xt_got, 1)

                tile_steps(v, step)
                if f == 0:
                    prepare_attention(v, put, own)
                for g in range(4):
                    v.wait_ge(gathered[g], (f + 1) * 8 * DMA)
                    for a in range(8 * g, 8 * g + 8):
                        v.scalar_tensor_tensor(out=x_sb[:, a, :], in0=gath[:, a, :], scalar=score[:, a:a + 1],
                                               in1=x_sb[:, a, :], op0=ALU.mult, op1=ALU.add).then_inc(moe_added, 1)
                    if f == 0:
                        v.wait_ge(moe_added, 8 * (g + 1))
                        moments(1, g)
                        if g > 0:
                            normalise(1, g - 1)
                        if g > 1:
                            take_values(v, g - 2)

            v.wait_ge(consts, CONSTS)
            square_gate()
            for g in range(4):
                v.wait_ge(x_in[g], DMA)
                moments(0, g)
                if g > 0:
                    normalise(0, g - 1)
                if g == 1:
                    prepare()
            normalise(0, 3)
            route(0)
            experts(0)
            normalise(1, 3)
            take_values(v, 2)
            take_values(v, 3)
            attention_dve(v, moments, normalise)
            normalise(2, 3)
            route(1)
            experts(1)

        @block.scalar
        def _(act):
            def gate(f):
                act.wait_ge(gate_sub, f + 2)
                act.activation(gexp[:], gtmp[:], ACT.Exp).then_inc(gate_exp, 1)

            def experts(f):
                base = f * NS

                def step(s, r, turn):
                    if runs(s, 1):
                        act.wait_ge(up_done, s + base)
                        if later(s, 3):
                            act.wait_ge(down_done, s + (base - 2))
                        for k in range(FK):
                            gelu = act.activation(hT[:, (r - 1) % 2, k, :], ps[:, 2 + (r - 1) % 2, k * P:(k + 1) * P], ACT.Gelu,
                                                  bias=w1_now[:, (r - 1) % 2, F + k:F + k + 1])
                        gelu.then_inc(gelu_done, 1)
                    if runs(s, 2):
                        act.wait_ge(down_done, s + (base - 1))
                        q = (r - 2) % 4
                        full = turn if r >= 2 else turn - 1
                        if not isinstance(full, int) or full > 0:
                            act.wait_ge(y_out[q], (full + f * per_ring(q)) * DMA)
                        act.copy(yr[:, q, :], ps[:, 6 + r % 2, 0:C]).then_inc(y_got, 1)
                        act.wait_ge(y_got, s + (base - 1))
                        act.dma_start(yslots[bass.ds((s - 2) * P, P), :], yr[:, q, :]).then_inc(y_out[q], DMA)

                tile_steps(act, step)

            take_transposes(act, 0)
            gate(0)
            experts(0)
            take_transposes(act, 1)
            attention_act(act)
            take_transposes(act, 2)
            gate(1)
            experts(1)

        @block.tensor
        def _(pe):
            def prepare():
                pe.wait_ge(consts, CONSTS)
                pe.wait_ge(gate_sub, 1)
                pe.transpose(ps[0:GD, 2, 0:E], wg_unit[:], ident[0:E, 0:E]).then_inc(wprep_pe, 1)
                pe.wait_ge(wprep_got, 1)
                pe.matmul(ps[:, 2, 0:E], wgred_in[:], wgT[:], start=True, stop=True).then_inc(wprep_pe, 1)
                pe.wait_ge(wprep_got, 2)
                pe.wait_ge(bias_i, 2 * DMA)
                pe.transpose(ps[:, 2, 0:E * FK], b1_in[:], ident[0:E * FK, 0:E * FK]).then_inc(wprep_pe, 1)
                pe.wait_ge(wprep_got, 3)

            def gate(f, n):
                def logits(g):
                    pe.wait_ge(zt_got, NG * n + g + 1)
                    for a in range(G4 * g, G4 * g + G4):
                        mm = pe.matmul(ps[:, 7, a * E:(a + 1) * E], zT[:, a * P:(a + 1) * P], wgate[:], start=True, stop=True)
                    return mm
                for g in transposes(pe, n):
                    if g >= 2:
                        logits(g - 2)
                logits(NG - 2)
                logits(NG - 1).then_inc(logits_done, 1)
                pe.wait_ge(onehot_done, f + 1)
                oh = onehot[:].rearrange("p a e -> p (a e)")
                pe.matmul(ps[:, 6, 0:NT * E], before[:], oh, start=True, stop=True)
                pe.matmul(ps[:, 6, NT * E:2 * NT * E], ones_bf[:], oh, start=True, stop=True).then_inc(counted, 1)

            def experts(f):
                base = f * NS
                pe.wait_ge(etab_done, f + 1)
                if f == 0:
                    pe.wait_ge(w2_in, DMA)
                    pe.wait_ge(bias_back, DMA)

                def step(s, r, turn):
                    if runs(s, 0):
                        pe.wait_ge(slot_in[r], (turn + (f * per_ring(r) + 1)) * DMA)
                        if later(s, 2):
                            pe.wait_ge(xt_got, s + (base - 1))
                        pe.transpose(ps[:, r % 2, 0:P], xin[:, r, :], ident[:]).then_inc(xt_put, 1)
                    if runs(s, 1):
                        b = 2 + (r - 1) % 2
                        pe.wait_ge(w1_got, s + base)
                        pe.wait_ge(xt_got, s + base)
                        if later(s, 3):
                            pe.wait_ge(gelu_done, s + (base - 2))
                        for k in range(FK):
                            mm = pe.matmul(ps[:, b, k * P:(k + 1) * P], w1_now[:, (r - 1) % 2, k * P:(k + 1) * P], xs[:, (r - 1) % 2, :],
                                           start=True, stop=True)
                        mm.then_inc(up_done, 1)
                    if runs(s, 2):
                        b = 6 + r % 2
                        e = pe.value_load(etab[0:1, bass.ds(s - 2, 1)], min_val=0, max_val=E - 1)
                        pe.wait_ge(gelu_done, s + (base - 1))
                        if later(s, 4):
                            pe.wait_ge(y_got, s + (base - 3))
                        for k in range(FK):
                            pe.matmul(ps[:, b, 0:C], hT[:, r % 2, k, :], w2_sb[:, bass.ds(e, 1), k, :].rearrange("p e c -> p (e c)"),
                                      start=(k == 0), stop=False)
                        pe.matmul(ps[:, b, 0:C], ones_bf[:], b2_rows[:, bass.ds(e * C, C)], start=False, stop=True).then_inc(down_done, 1)

                tile_steps(pe, step)

            prepare()
            gate(0, 0)
            experts(0)
            attention_pe_weights(pe)
            attention_pe(pe)
            gate(1, 2)
            experts(1)


_INS = ['L0_attn_x', 'L0_attn_w_attn', 'L0_attn_b_attn', 'L0_attn_la_attn', 'L0_attn_lb_attn', 'L0_attn_w_proj',
        'L0_attn_b_proj', 'L0_attn_la_proj', 'L0_attn_lb_proj', 'L0_ffn_wg_red', 'L0_ffn_wg', 'L0_ffn_w1',
        'L0_ffn_b1', 'L0_ffn_w2', 'L0_ffn_b2']


def kernel(**inputs):
    import numpy as _np
    import concourse.bacc as _bacc
    from concourse import mybir as _mybir
    from concourse.bass_utils import run_bass_kernel_spmd as _run

    nc = _bacc.Bacc("TRN2", target_bir_lowering=False, num_devices=1)
    arrays, args = {}, []
    for name in _INS:
        a = _np.ascontiguousarray(inputs[name])
        arrays[f"in_{name}_dram"] = a
        args.append(nc.dram_tensor(f"in_{name}_dram", a.shape, _mybir.dt.from_np(a.dtype), kind="ExternalInput").ap())
    shape = inputs["L0_attn_x"].shape
    args.append(nc.dram_tensor("out_0_dram", shape, _mybir.dt.float32, kind="ExternalOutput").ap())
    macaron_kernel(nc, *args)
    r = _run(nc, [arrays], core_ids=[0])
    return r.results[0]["out_0_dram"]
```
